# Optimizing a Trainium2 kernel written in Bass

```python
import numpy as np
import jax
import jax.numpy as jnp

def _softmax(x, axis=-1):
    return jax.nn.softmax(x, axis=axis)

def _gelu(x):
    return jax.nn.gelu(x, approximate=True)

def _silu(x):
    return jax.nn.silu(x)

def _sigmoid(x):
    return jax.nn.sigmoid(x)

def _layernorm(x, axis=-1, eps=1e-05):
    m = jnp.mean(x, axis=axis, keepdims=True)
    v = jnp.var(x, axis=axis, keepdims=True)
    return (x - m) / jnp.sqrt(v + eps)

def _scatter_add(tgt, idx, src, axis=0):
    return tgt.at[idx].add(src)

def _segment_sum(src, seg, n):
    return jax.ops.segment_sum(src, seg, n)
kernel_name = 'mk_decoder_postln_d1_seqx_r8_fe5fbf'

def setup_inputs(seed: int=0):
    np.random.seed(seed)
    _w = jnp.asarray

    def _rec_inputs():
        import jax
        import jax.numpy as jnp
        _rk = jax.random.key(seed)
        x = -0.0002928 + 1 * jax.random.normal(jax.random.fold_in(_rk, 1), (128, 64, 128), jnp.float32)
        _lenS = 64 - jax.random.randint(jax.random.fold_in(_rk, 7), (128,), 0, max(1, 64 // 4) + 1, jnp.int32)
        _lenS2 = 64 - jax.random.randint(jax.random.fold_in(_rk, 8), (128,), 0, max(1, 64 // 4) + 1, jnp.int32)
        _ctx_1024P = jax.random.normal(jax.random.fold_in(_rk, 11), (128, 16, 128), jnp.float32)
        _ctx_1024c = jax.random.dirichlet(jax.random.fold_in(_rk, 511), 0.3 * jnp.ones((16,), jnp.float32), (128, 64))
        _ctx_1024t = jnp.einsum('bsk,bkd->bsd', _ctx_1024c, _ctx_1024P)
        _ctx_1024t = _ctx_1024t * jax.lax.rsqrt(jnp.mean(jnp.square(_ctx_1024t)) + 1e-12) * 0.953939
        ctx_1024 = -1.39393e-06 + 0.999914 * (_ctx_1024t + 0.3 * jax.random.normal(jax.random.fold_in(_rk, 611), (128, 64, 128), jnp.float32))
        _validS = jnp.arange(64)[None, :] < _lenS[:, None]
        _validS2 = jnp.arange(64)[None, :] < _lenS2[:, None]
        _causal = jnp.tril(jnp.ones((64, 64), dtype=bool))
        mask_1x1xSxS2_ik0 = jnp.where(jnp.broadcast_to(_validS2[0:1, None, None, :], (1, 1, 64, 64)), 0, 1).astype(jnp.int32)
        return (x, ctx_1024, mask_1x1xSxS2_ik0)
    x, ctx_1024, mask_1x1xSxS2_ik0 = _rec_inputs()

    def _L0_attn_setup():
        import jax, jax.numpy as jnp
        import numpy as np
        B, S, H = (1, 256, 128)
        INTER, K, DST, DTR = (256, 4, 16, 64)

        def _ssm(dA, dBu, C):
            xs = (jnp.moveaxis(dA, 1, 0), jnp.moveaxis(dBu, 1, 0), jnp.moveaxis(C, 1, 0))
            state0 = jnp.zeros(dA.shape[:1] + dA.shape[2:], dA.dtype)

            def step(state, inp):
                Ai, dBui, Ci = inp
                state = Ai * state + dBui
                y = jnp.einsum('bhd,bd->bh', state, Ci)
                return (state, y)
            _, ys = jax.lax.scan(step, state0, xs)
            return jnp.moveaxis(ys, 0, 1)
        key = jax.random.key(seed)
        ks = jax.random.split(key, 10)
        sc = 0.02
        return {'x': jax.random.normal(ks[0], (B, S, H), jnp.float32), 'W_in': jax.random.normal(ks[1], (H, 2 * INTER), jnp.float32) * sc, 'conv_w': jax.random.normal(ks[2], (K, 1, INTER), jnp.float32) * sc, 'conv_b': jax.random.normal(ks[3], (INTER,), jnp.float32) * sc, 'W_x': jax.random.normal(ks[4], (INTER, DTR + 2 * DST), jnp.float32) * sc, 'W_dt': jax.random.normal(ks[5], (DTR, INTER), jnp.float32) * sc, 'b_dt': jax.random.normal(ks[6], (INTER,), jnp.float32) * sc, 'A_log': jax.random.normal(ks[7], (INTER, DST), jnp.float32) * sc, 'D': jax.random.normal(ks[8], (INTER,), jnp.float32) * sc, 'W_out': jax.random.normal(ks[9], (INTER, H), jnp.float32) * sc}
    _L0_attn_all = _L0_attn_setup()
    _L0_attn_in = {k: v for k, v in _L0_attn_all.items() if k in ('W_in', 'conv_w', 'conv_b', 'W_x', 'W_dt', 'b_dt', 'A_log', 'D', 'W_out')}
    del _L0_attn_all

    def _L0_xattn_setup():
        import jax, jax.numpy as jnp
        import numpy as np
        B, S, D, H = (2, 256, 128, 16)
        ND = D // H
        key = jax.random.key(seed)
        ks = jax.random.split(key, 11)
        scale = 1.0 / np.sqrt(D)
        inp = {'q': jax.random.normal(ks[0], (B, S, D), dtype=jnp.float32), 'k': jax.random.normal(ks[1], (B, S, D), dtype=jnp.float32), 'v': jax.random.normal(ks[2], (B, S, D), dtype=jnp.float32), 'mask': jnp.tril(jnp.ones((S, S), dtype=jnp.int32))[None, None, :, :], 'Wq': jax.random.normal(ks[3], (D, D), dtype=jnp.float32) * scale, 'bq': jnp.zeros((D,), dtype=jnp.float32), 'Wk': jax.random.normal(ks[4], (D, D), dtype=jnp.float32) * scale, 'bk': jnp.zeros((D,), dtype=jnp.float32), 'Wv': jax.random.normal(ks[5], (D, D), dtype=jnp.float32) * scale, 'bv': jnp.zeros((D,), dtype=jnp.float32), 'Wo': jax.random.normal(ks[6], (D, D), dtype=jnp.float32) * scale, 'bo': jnp.zeros((D,), dtype=jnp.float32)}
        return inp
    _L0_xattn_all = _L0_xattn_setup()
    _L0_xattn_in = {k: v for k, v in _L0_xattn_all.items() if k in ('Wq', 'bq', 'Wk', 'bk', 'Wv', 'bv', 'Wo', 'bo')}
    del _L0_xattn_all

    def _L0_ffn_setup():
        import jax, jax.numpy as jnp
        import numpy as np
        D_MODEL = 128
        key = jax.random.key(seed)
        k_x, k_w, k_a1, k_a2 = jax.random.split(key, 4)
        x = jax.random.normal(k_x, (4, 256, D_MODEL), dtype=jnp.float32)
        weight = jax.random.normal(k_w, (D_MODEL, D_MODEL), dtype=jnp.float32) * 0.02
        aux_weight1 = jax.random.normal(k_a1, (D_MODEL, D_MODEL), dtype=jnp.float32) * 0.02
        aux_weight2 = jax.random.normal(k_a2, (D_MODEL, D_MODEL), dtype=jnp.float32) * 0.02
        bias = jnp.zeros((D_MODEL,), dtype=jnp.float32)
        return {'x': x, 'weight': weight, 'aux_weight1': aux_weight1, 'aux_weight2': aux_weight2, 'bias': bias}
    _L0_ffn_all = _L0_ffn_setup()
    _L0_ffn_in = {k: v for k, v in _L0_ffn_all.items() if k in ('weight', 'aux_weight1', 'aux_weight2', 'bias')}
    del _L0_ffn_all
    return {'x': x, 'ctx_1024': ctx_1024, 'mask_1x1xSxS2_ik0': mask_1x1xSxS2_ik0, 'L0_attn_W_in': _L0_attn_in['W_in'], 'L0_attn_conv_w': _L0_attn_in['conv_w'], 'L0_attn_conv_b': _L0_attn_in['conv_b'], 'L0_attn_W_x': _L0_attn_in['W_x'], 'L0_attn_W_dt': _L0_attn_in['W_dt'], 'L0_attn_b_dt': _L0_attn_in['b_dt'], 'L0_attn_A_log': _L0_attn_in['A_log'], 'L0_attn_D': _L0_attn_in['D'], 'L0_attn_W_out': _L0_attn_in['W_out'], 'L0_xattn_Wq': _L0_xattn_in['Wq'], 'L0_xattn_bq': _L0_xattn_in['bq'], 'L0_xattn_Wk': _L0_xattn_in['Wk'], 'L0_xattn_bk': _L0_xattn_in['bk'], 'L0_xattn_Wv': _L0_xattn_in['Wv'], 'L0_xattn_bv': _L0_xattn_in['bv'], 'L0_xattn_Wo': _L0_xattn_in['Wo'], 'L0_xattn_bo': _L0_xattn_in['bo'], 'L0_ffn_weight': _L0_ffn_in['weight'], 'L0_ffn_aux_weight1': _L0_ffn_in['aux_weight1'], 'L0_ffn_aux_weight2': _L0_ffn_in['aux_weight2'], 'L0_ffn_bias': _L0_ffn_in['bias']}

def reference(x, ctx_1024, mask_1x1xSxS2_ik0, L0_attn_W_in, L0_attn_conv_w, L0_attn_conv_b, L0_attn_W_x, L0_attn_W_dt, L0_attn_b_dt, L0_attn_A_log, L0_attn_D, L0_attn_W_out, L0_xattn_Wq, L0_xattn_bq, L0_xattn_Wk, L0_xattn_bk, L0_xattn_Wv, L0_xattn_bv, L0_xattn_Wo, L0_xattn_bo, L0_ffn_weight, L0_ffn_aux_weight1, L0_ffn_aux_weight2, L0_ffn_bias):
    import jax
    import jax.numpy as jnp

    def _L0_attn_ref(x, W_in, conv_w, conv_b, W_x, W_dt, b_dt, A_log, D, W_out):
        import jax, jax.numpy as jnp
        import numpy as np
        B, S, H = (1, 256, 128)
        INTER, K, DST, DTR = (256, 4, 16, 64)

        def _ssm(dA, dBu, C):
            xs = (jnp.moveaxis(dA, 1, 0), jnp.moveaxis(dBu, 1, 0), jnp.moveaxis(C, 1, 0))
            state0 = jnp.zeros(dA.shape[:1] + dA.shape[2:], dA.dtype)

            def step(state, inp):
                Ai, dBui, Ci = inp
                state = Ai * state + dBui
                y = jnp.einsum('bhd,bd->bh', state, Ci)
                return (state, y)
            _, ys = jax.lax.scan(step, state0, xs)
            return jnp.moveaxis(ys, 0, 1)
        proj = x @ W_in
        raw, gate = jnp.split(proj, 2, axis=-1)
        conv = jax.lax.conv_general_dilated(raw, conv_w, window_strides=(1,), padding=[(K - 1, 0)], dimension_numbers=('NWC', 'WIO', 'NWC'), feature_group_count=INTER)
        h = jax.nn.silu(conv + conv_b)
        ssm_p = h @ W_x
        ts, Bmat, C = jnp.split(ssm_p, [DTR, DTR + DST], axis=-1)
        dt = jax.nn.softplus(ts @ W_dt + b_dt)
        A = -jnp.exp(A_log)
        dA = jnp.exp(dt[..., None] * A)
        dBu = dt[..., None] * Bmat[:, :, None, :] * h[..., None]
        y = _ssm(dA, dBu, C)
        y = y + h * D
        y = y * jax.nn.silu(gate)
        return y @ W_out

    def _L0_xattn_ref(q, k, v, mask, Wq, bq, Wk, bk, Wv, bv, Wo, bo):
        import jax, jax.numpy as jnp
        import numpy as np
        B, S, D, H = (2, 256, 128, 16)
        ND = D // H
        batch, seq_len, _ = q.shape
        qh = (q @ Wq.T + bq).reshape(batch, seq_len, H, ND).transpose(0, 2, 1, 3)
        kh = (k @ Wk.T + bk).reshape(batch, seq_len, H, ND).transpose(0, 2, 1, 3)
        vh = (v @ Wv.T + bv).reshape(batch, seq_len, H, ND).transpose(0, 2, 1, 3)
        score = jnp.einsum('bhqd,bhkd->bhqk', qh, kh) / jnp.sqrt(jnp.float32(ND))
        score = jnp.where(mask == 0, jnp.float32(-1000000000.0), score)
        score = jax.nn.softmax(score, axis=-1)
        out = jnp.einsum('bhqk,bhkd->bhqd', score, vh)
        out = out.transpose(0, 2, 1, 3).reshape(batch, seq_len, D)
        return out @ Wo.T + bo

    def _L0_ffn_ref(x, weight, aux_weight1, aux_weight2, bias):
        import jax, jax.numpy as jnp
        import numpy as np
        D_MODEL = 128
        h = jnp.einsum('btc,cd->btd', x, weight)
        h = jnp.einsum('btc,cd->btd', h, aux_weight1)
        h = jnp.einsum('btc,cd->btd', h, aux_weight2)
        return jnp.tanh(h + bias)
    x = _layernorm(x + _L0_attn_ref(x, L0_attn_W_in, L0_attn_conv_w, L0_attn_conv_b, L0_attn_W_x, L0_attn_W_dt, L0_attn_b_dt, L0_attn_A_log, L0_attn_D, L0_attn_W_out), axis=-1)
    x = _layernorm(x + _L0_xattn_ref(x, ctx_1024, ctx_1024, mask_1x1xSxS2_ik0, L0_xattn_Wq, L0_xattn_bq, L0_xattn_Wk, L0_xattn_bk, L0_xattn_Wv, L0_xattn_bv, L0_xattn_Wo, L0_xattn_bo), axis=-1)
    x = _layernorm(x + _L0_ffn_ref(x, L0_ffn_weight, L0_ffn_aux_weight1, L0_ffn_aux_weight2, L0_ffn_bias), axis=-1)
    return x

_drawn_inputs = setup_inputs


def setup_inputs(seed=0):
    import zlib

    import numpy as np

    out = dict(_drawn_inputs(seed))
    spreads = {'L0_xattn_bq': (0.0, 0.296),
     'L0_xattn_bk': (0.0, 0.8),
     'L0_xattn_bv': (0.0, 0.1),
     'L0_xattn_bo': (0.0, 0.1),
     'L0_ffn_bias': (0.0, 0.1)}
    factors = {'L0_attn_W_in': 8.0,
     'L0_attn_conv_w': 8.0,
     'L0_attn_conv_b': 8.0,
     'L0_attn_W_x': 8.0,
     'L0_attn_W_dt': 8.0,
     'L0_attn_b_dt': 8.0,
     'L0_attn_A_log': 8.0,
     'L0_attn_D': 8.0,
     'L0_attn_W_out': 8.0,
     'L0_ffn_weight': 5.04,
     'L0_ffn_aux_weight1': 4.962,
     'L0_ffn_aux_weight2': 5.048}
    for name, (base, spread) in spreads.items():
        noise = np.random.default_rng([zlib.crc32(name.encode()), seed]).standard_normal(out[name].shape)
        drawn = base * np.exp(spread * noise) if base else spread * noise
        out[name] = jnp.asarray(drawn.astype(out[name].dtype))
    for name, factor in factors.items():
        out[name] = (out[name] * factor).astype(out[name].dtype)
    return out
```

```python
import numpy as np
import concourse.bass as bass
from concourse import mybir
from contextlib import ExitStack


def decoder_layer(nc, t, out_dram):
    F32, BF16, I32 = mybir.dt.float32, mybir.dt.bfloat16, mybir.dt.int32
    ALU, ACT, AX = mybir.AluOpType, mybir.ActivationFunctionType, mybir.AxisListType

    B, S, D = t["x"].shape
    P = 128
    NB = 8
    R = NB * S
    G = B // NB
    NP = R // P
    CH = t["L0_attn_W_out"].shape[0]
    NH2 = CH // P
    NS = t["L0_attn_A_log"].shape[1]
    KC = t["L0_attn_conv_w"].shape[0]
    DTR = t["L0_attn_W_dt"].shape[0]
    SSP = DTR + 2 * NS
    H = 16
    HD = D // H
    HP = H // 2
    SP_ = KC - 1 + S
    VW = HD + 1
    EPS = 1e-5
    NEG = -1.0e30
    QSCALE = float(HD) ** -0.5
    assert R == 512 and NH2 == 2 and NP == 4 and SSP == 96 and SSP - DTR == 32

    JOBS = [("xtr", 6, "A"), ("outp", 7, "T"), ("raw0", 6, "A"), ("raw1", 7, "A"), ("ctr", 6, "A"),
            ("kT", 7, "A"), ("gate0", 6, "A"), ("gate1", 7, "A"), ("x1tr", 6, "T"), ("qT", 7, "T"),
            ("ssp", 6, "A"), ("dt0", 7, "A"), ("dt1", 6, "A"), ("pv0", 7, "T"), ("pv1", 6, "T"),
            ("pv2", 7, "T"), ("pv3", 6, "T"), ("v", 7, "A")]
    TAIL = {1: "atr", 3: "wo", 7: "x2tr", 9: "ffn"}
    AHEAD = 3
    JOBS += [(f"B{n}", 7, "A") for n in range(AHEAD)]
    for n in range(NS):
        if n + AHEAD < NS:
            JOBS.append((f"B{n + AHEAD}", 7, "A"))
        if n in TAIL:
            JOBS.append((TAIL[n], 7, "T"))

    def numbers(name, it):
        kinds = "A" if isinstance(it, int) and it == 0 else "T" if isinstance(it, int) and it == G else "AT"
        here = [j for j in JOBS if j[2] in kinds]
        pos = [j[0] for j in here].index(name)
        bank = here[pos][1]
        same = sum(j[1] == bank for j in here[:pos + 1])
        if isinstance(it, int) and it == 0:
            return bank, pos + 1, same
        first = [j for j in JOBS if j[2] == "A"]
        return (bank, (it - 1) * len(JOBS) + len(first) + pos + 1,
                (it - 1) * sum(j[1] == bank for j in JOBS) + sum(j[1] == bank for j in first) + same)

    def wait(eng, semaphore, value):
        if not (isinstance(value, int) and value <= 0):
            eng.wait_ge(semaphore, value)

    ctx = ExitStack()
    with ctx:
        def sb(name, shape, dt=F32):
            return ctx.enter_context(nc.sbuf_tensor(name, shape, dt))

        def sem(name):
            return ctx.enter_context(nc.semaphore(name))

        ident = sb("ident", [P, P])
        identb = sb("identb", [P, P], BF16)
        sel = sb("sel", [SSP, 2 * NS, P], BF16)
        mhalf = sb("mhalf", [P, NP])
        maski = sb("maski", [P, S], I32)
        maskneg = sb("maskneg", [P, S], BF16)
        w_in = sb("w_in", [P, 2 * CH])
        conv_w = sb("conv_w", [P, KC, NH2])
        conv_b = sb("conv_b", [P, NH2])
        w_x = sb("w_x", [P, NH2, SSP])
        w_dt = sb("w_dt", [SSP, CH])
        b_dt = sb("b_dt", [P, NH2])
        a_neg = sb("a_neg", [P, NH2, NS])
        d_skip = sb("d_skip", [P, NH2])
        w_out = sb("w_out", [P, NH2, D])
        wraw = sb("wraw", [P, 7, D])
        wT = sb("wT", [P, 6, D])
        w_ffn = sb("w_ffn", [P, 2, D])
        bq = sb("bq", [P, 1])
        bk = sb("bk", [P, 1])
        bv = sb("bv", [P, D])
        bo = sb("bo", [P, D])
        bf = sb("bf", [P, D])
        x_in = sb("x_in", [P, NP, D])
        ctx_in = sb("ctx_in", [P, NP, D])
        xT = sb("xT", [P, R])
        ctxT = sb("ctxT", [P, R])
        kT = sb("kT", [P, NB, S])
        k_bd = sb("k_bd", [P, NB, H, S])
        v_bd = sb("v_bd", [P, NB, HP, 2 * VW])
        rawp = sb("rawp", [P, NH2, NB, SP_])
        xc = sb("xc", [P, NH2, R])
        th = sb("th", [P, NH2, R])
        h = sb("h", [P, NH2, R])
        tg = sb("tg", [P, NH2, R])
        sg = sb("sg", [P, NH2, R])
        ssp = sb("ssp", [SSP, R])
        bc3 = sb("bc3", [SSP, R], BF16)
        rest = sb("rest", [32, R])
        mid = sb("mid", [32, R], BF16)
        z = sb("z", [P, NH2, R])
        az = sb("az", [P, NH2, R])
        zr = sb("zr", [P, NH2, R])
        dt = sb("dt", [P, NH2, R])
        u = sb("u", [P, NH2, R])
        b_all = sb("b_all", [P, AHEAD + 1, R])
        dbu = sb("dbu", [P, 2, NH2 * R])
        st = sb("st", [P, 3, NH2 * R])
        cs = sb("cs", [P, 2, NH2 * R])
        yg = sb("yg", [P, NH2, R])
        x_res = sb("x_res", [P, NP, D])
        r = sb("r", [P, NP, D])
        stats = sb("stats", [P, NP, 6])
        mv = sb("mv", [P, NP, 2])
        rstd = sb("rstd", [P, 2, NP])
        x1 = sb("x1", [P, NP, D])
        x1b = sb("x1b", [P, NP, D])
        x1T = sb("x1T", [P, R])
        qT = sb("qT", [P, R])
        nmax = sb("nmax", [P, 2, H])
        pr = sb("pr", [P, 2, H * S])
        prT = sb("prT", [P, 2, HP * P])
        rden = sb("rden", [P, 2, H])
        att = sb("att", [P, NP, D])
        attT = sb("attT", [P, R])
        r2 = sb("r2", [P, NP, D])
        x2 = sb("x2", [P, NP, D])
        x2T = sb("x2T", [P, R])
        f = sb("f", [P, NP, D])
        o = sb("o", [P, NP, D])
        ps = ctx.enter_context(nc.psum_tensor("ps", [P, 8, 512], F32))

        C_BANK, Y_BANK, PT_BANK = 4, 5, 4
        da = [ps[:, 2 * i:2 * i + 2, :] for i in range(2)]
        sc = [ps[:, 2 * i:2 * i + 2, :] for i in range(2)]

        consts_in = sem("consts_in")
        x_loaded, ctx_loaded, xres_loaded = sem("x_loaded"), sem("ctx_loaded"), sem("xres_loaded")
        kbd_loaded = sem("kbd_loaded")
        stored = sem("stored")
        pool_const, act_const, dve_const, pe_const = (sem("pool_const"), sem("act_const"), sem("dve_const"),
                                                      sem("pe_const"))
        work_ready = sem("work_ready")
        sc_ready = sem("sc_ready")
        pt_ready = sem("pt_ready")
        c_ready = sem("c_ready")
        y_added = sem("y_added")
        bank_read = {6: sem("bank6_read"), 7: sem("bank7_read")}
        th_ready = sem("th_ready")
        tg_ready = sem("tg_ready")
        sp_step = sem("sp_step")
        split_act = sem("split_act")
        exp_ready = sem("exp_ready")
        pr_ready = sem("pr_ready")
        pt_act = sem("pt_act")
        f_ready = sem("f_ready")
        dve_a = sem("dve_a")
        dve_t = sem("dve_t")
        xc_ready = sem("xc_ready")
        h_ready = sem("h_ready")
        split_dve = sem("split_dve")
        zr_ready = sem("zr_ready")
        da_clear = sem("da_clear")
        scanned = sem("scanned")
        cs_ready = sem("cs_ready")
        yg_ready = sem("yg_ready")
        ln_stats = sem("ln_stats")
        x1_ready = sem("x1_ready")
        sm_ready = sem("sm_ready")
        pt_dve = sem("pt_dve")
        x2_ready, fin_ready, o_ready = sem("x2_ready"), sem("fin_ready"), sem("o_ready")
        dt_ready = sem("dt_ready")
        u_ready = sem("u_ready")
        dbu_ready = sem("dbu_ready")
        rstd_ready = sem("rstd_ready")
        x1b_ready = sem("x1b_ready")

        x_rows = t["x"].rearrange("(g i b) s d -> g (b s) i d", g=G, i=NP)
        ctx_rows = t["ctx_1024"].rearrange("(g i b) s d -> g (b s) i d", g=G, i=NP)
        out_rows = out_dram.rearrange("(g i b) s d -> g (b s) i d", g=G, i=NP)

        def over_groups(eng, iteration):
            iteration(0, True, False)
            with eng.Fori(1, G) as it:
                iteration(it, True, True)
            iteration(G, False, True)

        block = ctx.enter_context(nc.Block())

        @block.sync
        def _(sp):
            col = lambda a: a.rearrange("(p o) -> p o", o=1)
            row = lambda a: a.rearrange("(o n) -> o n", o=1).to_broadcast([P, D])
            loads = [(w_in[:, :], t["L0_attn_W_in"]),
                     (w_x[:, :, :], t["L0_attn_W_x"].rearrange("(c p) n -> p c n", p=P)),
                     (w_dt[0:DTR, :], t["L0_attn_W_dt"]),
                     (conv_b[:, :], t["L0_attn_conv_b"].rearrange("(c p) -> p c", p=P)),
                     (b_dt[:, :], t["L0_attn_b_dt"].rearrange("(c p) -> p c", p=P)),
                     (d_skip[:, :], t["L0_attn_D"].rearrange("(c p) -> p c", p=P)),
                     (a_neg[:, :, :], t["L0_attn_A_log"].rearrange("(c p) n -> p c n", p=P)),
                     (w_out[:, :, :], t["L0_attn_W_out"].rearrange("(c p) n -> p c n", p=P)),
                     (bq[:, :], col(t["L0_xattn_bq"])), (bk[:, :], col(t["L0_xattn_bk"])),
                     (bv[:, :], row(t["L0_xattn_bv"])), (bo[:, :], row(t["L0_xattn_bo"])),
                     (bf[:, :], row(t["L0_ffn_bias"])),
                     (maski[0:S, :], t["mask_1x1xSxS2_ik0"][0, 0]),
                     (maski[S:2 * S, :], t["mask_1x1xSxS2_ik0"][0, 0])]
            loads += [(conv_w[:, k, :], t["L0_attn_conv_w"][k, 0].rearrange("(c p) -> p c", p=P)) for k in range(KC)]
            loads += [(wraw[:, i, :], t[n]) for i, n in enumerate(
                ("L0_xattn_Wq", "L0_xattn_Wk", "L0_xattn_Wv", "L0_xattn_Wo",
                 "L0_ffn_weight", "L0_ffn_aux_weight1", "L0_ffn_aux_weight2"))]
            assert len(loads) == N_CONSTS
            with nc.allow_non_contiguous_dma(reason="channels of small vectors go to the partitions"):
                for dst, src in loads:
                    sp.dma_start(dst, src).then_inc(consts_in, 16)

            def iteration(it, do_a, do_t):
                if do_a:
                    sp.dma_start(x_in[:, :, :], x_rows[it]).then_inc(x_loaded, 16)
                    sp.dma_start(ctx_in[:, :, :], ctx_rows[it]).then_inc(ctx_loaded, 16)
                    if do_t:
                        sp.wait_ge(sc_ready, it * NP)
                    else:
                        sp.wait_ge(bank_read[7], numbers("kT", it)[2])
                        sp.wait_ge(pool_const, POOL_CONSTS)
                    for hh in range(H):
                        sp.dma_start(k_bd[hh * HD:(hh + 1) * HD, :, hh, :],
                                     kT[hh * HD:(hh + 1) * HD, :, :]).then_inc(kbd_loaded, 16)
                    sp.dma_start(x_res[:, :, :], x_rows[it]).then_inc(xres_loaded, 16)
                if do_t:
                    sp.wait_ge(o_ready, it)
                    sp.dma_start(out_rows[it - 1], o[:, :, :]).then_inc(stored, 16)

            over_groups(sp, iteration)
            sp.wait_ge(stored, (G + 1) * 16)

        @block.tensor
        def _(pe):
            mm = nc.tensor.matmul

            def job(name, it):
                bank, _, read = numbers(name, it)
                wait(pe, bank_read[bank], read - 1)
                return ps[:, bank, :]

            def wait_read(name, it):
                bank, _, read = numbers(name, it)
                pe.wait_ge(bank_read[bank], read)

            def transposes(bank, src, it):
                for i in range(NP):
                    last = nc.tensor.transpose(bank[:, i * P:(i + 1) * P], src[:, i, :], ident[:, :])
                last.then_inc(work_ready, 1)

            pe.wait_ge(consts_in, N_CONSTS * 16)
            pe.wait_ge(pool_const, POOL_CONSTS)
            for i in range(6):
                last = nc.tensor.transpose(ps[:, i // 4, (i % 4) * P:(i % 4 + 1) * P], wraw[:, i, :], ident[:, :])
            last.then_inc(pe_const, 1)
            pe.wait_ge(act_const, 3)
            mm(ps[:, 2, 0:D], wT[:, 5, :], wraw[:, 6, :], start=True, stop=True).then_inc(pe_const, 1)
            pe.wait_ge(act_const, 4)
            mm(ps[:, 3, 0:D], wT[:, 4, :], w_ffn[:, 0, :], start=True, stop=True).then_inc(pe_const, 1)
            pe.wait_ge(act_const, ACT_CONSTS)
            pe.wait_ge(dve_const, DVE_CONSTS)

            def scores(i, it):
                if i >= 2:
                    pe.wait_ge(sm_ready, (it - 1) * NP + i - 1)
                else:
                    pe.wait_ge(scanned, it * NS)
                if i == 0:
                    wait_read("qT", it)
                    pe.wait_ge(kbd_loaded, it * H * 16)
                bank = sc[i % 2]
                for c in range(2):
                    mm(bank[:, c, :], identb[:, :],
                       maskneg[:, :].unsqueeze(1).to_broadcast([P, H // 2, S]),
                       start=True, stop=False, skip_group_check=True)
                for c in range(2):
                    for b in range(2):
                        last = mm(bank[b * S:(b + 1) * S, c, :], qT[:, (2 * i + b) * S:(2 * i + b + 1) * S],
                                  k_bd[:, 2 * i + b, c * H // 2:(c + 1) * H // 2, :],
                                  start=False, stop=True, skip_group_check=True)
                last.then_inc(sc_ready, 1)

            def transpose_probs(i, it):
                pe.wait_ge(pr_ready, (it - 1) * NP + i + 1)
                if i == 0:
                    pe.wait_ge(cs_ready, it * NS)
                    pe.wait_ge(yg_ready, it)
                else:
                    pe.wait_ge(pt_act, (it - 1) * NP + i)
                    pe.wait_ge(pt_dve, (it - 1) * NP + i)
                for c in range(HP):
                    last = nc.tensor.transpose(ps[:, PT_BANK + c // 4, (c % 4) * P:(c % 4 + 1) * P],
                                               pr[:, i % 2, c * P:(c + 1) * P], ident[:, :])
                last.then_inc(pt_ready, 1)

            def weigh_values(i, it):
                bank = job(f"pv{i}", it)
                pe.wait_ge(pt_act, (it - 1) * NP + i + 1)
                pe.wait_ge(pt_dve, (it - 1) * NP + i + 1)
                for c in range(HP):
                    for b in range(2):
                        last = mm(bank[b * S:(b + 1) * S, c * 2 * VW:(c + 1) * 2 * VW],
                                  prT[:, i % 2, c * P + b * S:c * P + (b + 1) * S],
                                  v_bd[:, 2 * i + b, c, :], start=True, stop=True, skip_group_check=True)
                last.then_inc(work_ready, 1)

            def to_b(n, it):
                mm(job(f"B{n}", it), sel[:, n, :], bc3[:, :], start=True, stop=True).then_inc(work_ready, 1)

            def add_y(n, it):
                pe.wait_ge(cs_ready, it * NS + n + 1)
                for c in range(NH2):
                    last = mm(ps[:, Y_BANK + c, :], ident[:, :], cs[:, n % 2, c * R:(c + 1) * R],
                              start=n == 0, stop=n == NS - 1, skip_group_check=True)
                last.then_inc(y_added, 1)

            def iteration(it, do_a, do_t):
                if do_a:
                    pe.wait_ge(x_loaded, (it + 1) * 16)
                    bank = job("xtr", it)
                    wait(pe, yg_ready, it)
                    transposes(bank, x_in, it)
                if do_t:
                    bank = job("outp", it)
                    pe.wait_ge(yg_ready, it)
                    for i in range(NP):
                        for c in range(NH2):
                            last = mm(bank[:, i * D:(i + 1) * D], yg[:, c, i * P:(i + 1) * P], w_out[:, c, :],
                                      start=c == 0, stop=c == NH2 - 1)
                    last.then_inc(work_ready, 1)
                if do_a:
                    wait_read("xtr", it)
                    for c in range(NH2):
                        mm(job(f"raw{c}", it), w_in[:, c * P:(c + 1) * P], xT[:, :],
                           start=True, stop=True).then_inc(work_ready, 1)
                    pe.wait_ge(ctx_loaded, (it + 1) * 16)
                    transposes(job("ctr", it), ctx_in, it)
                    wait_read("ctr", it)
                    mm(job("kT", it), wT[:, 1, :], ctxT[:, :], start=True, stop=True).then_inc(work_ready, 1)
                    for c in range(NH2):
                        mm(job(f"gate{c}", it), w_in[:, CH + c * P:CH + (c + 1) * P], xT[:, :],
                           start=True, stop=True).then_inc(work_ready, 1)
                if do_t:
                    pe.wait_ge(x1_ready, it)
                    transposes(job("x1tr", it), x1, it)
                    wait_read("x1tr", it)
                    mm(job("qT", it), wT[:, 0, :], x1T[:, :], start=True, stop=True).then_inc(work_ready, 1)
                    scores(0, it)
                    scores(1, it)
                if do_a:
                    bank = job("ssp", it)
                    pe.wait_ge(h_ready, it + 1)
                    for c in range(NH2):
                        last = mm(bank[0:SSP, :], w_x[:, c, :], h[:, c, :], start=c == 0, stop=c == NH2 - 1)
                    last.then_inc(work_ready, 1)
                if do_t:
                    transpose_probs(0, it)
                if do_a:
                    wait_read("ssp", it)
                    for c in range(NH2):
                        mm(job(f"dt{c}", it), w_dt[:, c * P:(c + 1) * P], ssp[:, :],
                           start=True, stop=True).then_inc(work_ready, 1)
                if do_t:
                    for i in range(NP):
                        if i + 2 < NP:
                            scores(i + 2, it)
                        if i + 1 < NP:
                            transpose_probs(i + 1, it)
                        weigh_values(i, it)
                if do_a:
                    bank = job("v", it)
                    for b in range(NB):
                        for e in range(2):
                            last = mm(bank[e * S:(e + 1) * S, b * HP * HD:(b + 1) * HP * HD],
                                      ctxT[:, b * S:(b + 1) * S],
                                      wT[:, 2, :].rearrange("p (c e d) -> p c e d", e=2, d=HD)[:, :, e, :],
                                      start=True, stop=True, skip_group_check=True)
                    last.then_inc(work_ready, 1)
                    pe.wait_ge(split_act, (it + 1) * 3)
                    pe.wait_ge(split_dve, (it + 1) * 2)
                    for n in range(AHEAD):
                        to_b(n, it)

                def tail(n):
                    if n == 1:
                        bank = job("atr", it)
                        wait_read("pv2", it)
                        wait_read("pv3", it)
                        transposes(bank, att, it)
                    if n == 3:
                        bank = job("wo", it)
                        wait_read("atr", it)
                        for i in range(NP):
                            last = mm(bank[:, i * D:(i + 1) * D], attT[:, i * P:(i + 1) * P], wT[:, 3, :],
                                      start=True, stop=True)
                        last.then_inc(work_ready, 1)
                    if n == 7:
                        bank = job("x2tr", it)
                        pe.wait_ge(x2_ready, it)
                        transposes(bank, x2, it)
                    if n == 9:
                        bank = job("ffn", it)
                        wait_read("x2tr", it)
                        for i in range(NP):
                            last = mm(bank[:, i * D:(i + 1) * D], x2T[:, i * P:(i + 1) * P], w_ffn[:, 1, :],
                                      start=True, stop=True)
                        last.then_inc(work_ready, 1)

                for n in range(NS):
                    if do_a:
                        if n + AHEAD < NS:
                            to_b(n + AHEAD, it)
                        if n > 0:
                            pe.wait_ge(cs_ready, it * NS + n)
                        else:
                            wait(pe, pt_act, it * NP)
                            wait(pe, pt_dve, it * NP)
                        mm(ps[:, C_BANK, :], sel[:, NS + n, :], bc3[:, :], start=True, stop=True).then_inc(c_ready, 1)
                        if n > 0:
                            if n == 1:
                                wait_read("pv3" if do_t else "dt1", it)
                            add_y(n - 1, it)
                    if do_t:
                        tail(n)
                if do_a:
                    add_y(NS - 1, it)

            over_groups(pe, iteration)

        @block.scalar
        def _(act):
            A = nc.scalar.activation

            def wait_ready(name, it):
                bank, ready, _ = numbers(name, it)
                act.wait_ge(work_ready, ready)
                return ps[:, bank, :], bank_read[bank]

            act.wait_ge(consts_in, N_CONSTS * 16)
            A(a_neg[:, :, :], a_neg[:, :, :], ACT.Exp).then_inc(act_const, 1)
            act.wait_ge(pe_const, 1)
            A(wT[:, 0:4, :], ps[:, 0, :].rearrange("p (i d) -> p i d", i=4), ACT.Copy).then_inc(act_const, 1)
            A(wT[:, 4:6, :], ps[:, 1, 0:2 * D].rearrange("p (i d) -> p i d", i=2), ACT.Copy).then_inc(act_const, 1)
            act.wait_ge(pe_const, 2)
            A(w_ffn[:, 0, :], ps[:, 2, 0:D], ACT.Copy).then_inc(act_const, 1)
            act.wait_ge(pe_const, 3)
            A(w_ffn[:, 1, :], ps[:, 3, 0:D], ACT.Copy).then_inc(act_const, 1)
            A(w_in[:, CH:2 * CH], w_in[:, CH:2 * CH], ACT.Copy, scale=0.5).then_inc(act_const, 1)
            A(bq[:, :], bq[:, :], ACT.Copy, scale=QSCALE).then_inc(act_const, 1)
            act.wait_ge(act_const, ACT_CONSTS)
            act.wait_ge(dve_const, DVE_CONSTS)
            act.wait_ge(pool_const, POOL_CONSTS)

            def read(name, it, dst, func=ACT.Copy, **kw):
                src, done = wait_ready(name, it)
                if len(dst.shape) == 3:
                    src = src.rearrange("p (i d) -> p i d", i=dst.shape[1])
                A(dst, src, func, **kw).then_inc(done, 1)

            def softmax_exp(i, it):
                act.wait_ge(sm_ready, (it - 1) * NP + i + 1)
                A(pr[:, i % 2, :], pr[:, i % 2, :], ACT.Exp).then_inc(pr_ready, 1)

            def copy_probs(i, it):
                act.wait_ge(pt_ready, (it - 1) * NP + i + 1)
                if i >= 2:
                    act.wait_ge(work_ready, numbers(f"pv{i - 2}", it)[1])
                A(prT[:, i % 2, 0:4 * P], ps[:, PT_BANK, :], ACT.Copy).then_inc(pt_act, 1)

            def iteration(it, do_a, do_t):
                if do_a:
                    read("xtr", it, xT[:, :])
                    for c in range(NH2):
                        src, done = wait_ready(f"raw{c}", it)
                        A(rawp[:, c, :, KC - 1:], src.rearrange("p (b s) -> p b s", b=NB), ACT.Copy).then_inc(done, 1)
                    read("ctr", it, ctxT[:, :])
                    wait(act, kbd_loaded, it * H * 16)
                    src, done = wait_ready("kT", it)
                    A(kT[:, :, :], src.rearrange("p (b s) -> p b s", b=NB), ACT.Identity,
                      bias=bk[:, 0:1]).then_inc(done, 1)
                    for c in range(NH2):
                        src, _ = wait_ready(f"gate{c}", it)
                        A(tg[:, c, :], src, ACT.Tanh).then_inc(tg_ready, 1)
                    act.wait_ge(xc_ready, (it + 1) * 2)
                    A(th[:, :, :], xc[:, :, :], ACT.Tanh).then_inc(th_ready, 1)
                if do_t:
                    read("x1tr", it, x1T[:, :])
                    read("qT", it, qT[:, :], ACT.Identity, bias=bq[:, 0:1], scale=QSCALE)
                if do_a:
                    bank, ready, _ = numbers("ssp", it)
                    act.wait_ge(work_ready, ready)
                    A(ssp[:, :], ps[0:SSP, bank, :], ACT.Copy).then_inc(bank_read[bank], 1)
                    act.wait_ge(bank_read[bank], numbers("ssp", it)[2])
                    A(bc3[0:32, :], ssp[DTR:SSP, :], ACT.Copy).then_inc(split_act, 1)
                    act.wait_ge(split_dve, it * 2 + 1)
                    A(mid[:, :], rest[:, :], ACT.Copy).then_inc(split_act, 1)
                    A(bc3[32:64, :], rest[:, :], ACT.Copy).then_inc(split_act, 1)
                if do_t:
                    softmax_exp(0, it)
                if do_a:
                    for c in range(NH2):
                        read(f"dt{c}", it, z[:, c, :], ACT.Identity, bias=b_dt[:, c:c + 1])
                    act.wait_ge(bank_read[7], numbers("dt0", it)[2])
                    act.wait_ge(bank_read[6], numbers("dt1", it)[2])
                    A(az[:, :, :], z[:, :, :], ACT.Abs).then_inc(sp_step, 1)
                    act.wait_ge(sp_step, it * 3 + 1)
                    A(az[:, :, :], az[:, :, :], ACT.Exp, scale=-1.0).then_inc(sp_step, 1)
                    act.wait_ge(sp_step, it * 3 + 2)
                    A(az[:, :, :], az[:, :, :], ACT.Ln, bias=1.0).then_inc(sp_step, 1)
                if do_t:
                    copy_probs(0, it)
                    for i in range(1, NP):
                        softmax_exp(i, it)
                        copy_probs(i, it)

                def tail(n):
                    if n == 4:
                        read("atr", it, attT[:, :])
                    if n == 6:
                        read("wo", it, r2[:, :, :])
                    if n == 10:
                        read("x2tr", it, x2T[:, :])
                    if n == 12:
                        read("ffn", it, f[:, :, :])
                    if n == 14:
                        act.wait_ge(fin_ready, it)
                        A(f[:, :, :], f[:, :, :], ACT.Tanh).then_inc(f_ready, 1)

                def copy_b(n):
                    if n > AHEAD:
                        act.wait_ge(dbu_ready, it * NS + n - AHEAD)
                    read(f"B{n}", it, b_all[:, n % (AHEAD + 1), :])

                if do_a:
                    for n in range(AHEAD):
                        copy_b(n)
                    act.wait_ge(dt_ready, it + 1)
                    act.wait_ge(da_clear, it + 1)
                for n in range(NS):
                    if do_a:
                        if n >= 2:
                            act.wait_ge(scanned, it * NS + n - 1)
                        for c in range(NH2):
                            A(da[n % 2][:, c, :].rearrange("p (b s) -> p b s", b=NB)[:, :, 1:],
                              dt[:, c, :].rearrange("p (b s) -> p b s", b=NB)[:, :, 1:],
                              ACT.Exp, scale=a_neg[:, c, n:n + 1]).then_inc(exp_ready, 1)
                    if do_t:
                        tail(n)
                    if do_a and AHEAD <= n + 1 < NS:
                        copy_b(n + 1)

            over_groups(act, iteration)

        @block.vector
        def _(dve):
            V = nc.vector
            count = {}

            def wait_ready(name, it):
                bank, ready, _ = numbers(name, it)
                dve.wait_ge(work_ready, ready)
                return ps[:, bank, :], bank_read[bank]

            dve.wait_ge(consts_in, N_CONSTS * 16)
            V.tensor_scalar(maskneg[:, :], maski[:, :], 0, NEG, ALU.is_equal, ALU.mult).then_inc(dve_const, 1)
            V.tensor_scalar(conv_w[:, :, :], conv_w[:, :, :], 0.5, None, ALU.mult).then_inc(dve_const, 1)
            V.tensor_scalar(conv_b[:, :], conv_b[:, :], 0.5, None, ALU.mult).then_inc(dve_const, 1)
            dve.wait_ge(act_const, ACT_CONSTS)
            V.tensor_scalar(a_neg[:, :, :], a_neg[:, :, :], -1.0, None, ALU.mult).then_inc(dve_const, 1)
            dve.wait_ge(pool_const, POOL_CONSTS)
            V.tensor_copy(identb[:, :], ident[:, :]).then_inc(dve_const, 1)
            V.memset(o[:, :, :], 0.0).then_inc(stored, 16)
            V.memset(w_dt[DTR:SSP, :], 0.0).then_inc(dve_const, 1)
            for e in range(2):
                V.memset(v_bd[e * S:(e + 1) * S, :, :, e * VW + HD:e * VW + HD + 1], 1.0).then_inc(dve_const, 1)
            for j in range(3):
                V.tensor_copy(sel[32 * j:32 * j + 32, :, :],
                              ident[32 * j:32 * j + 32, 32 * j:32 * j + 32].unsqueeze(2)
                              .to_broadcast([32, 32, P])).then_inc(dve_const, 1)
            dve.wait_ge(dve_const, DVE_CONSTS)

            def batches(ap):
                return ap.rearrange("p (b s) -> p b s", b=NB)

            def iteration(it, do_a, do_t):
                count["a"] = count["t"] = 0

                def step_a(ins):
                    count["a"] += 1
                    ins.then_inc(dve_a, 1)
                    dve.wait_ge(dve_a, it * DVE_A + count["a"])

                def step_t(ins):
                    count["t"] += 1
                    ins.then_inc(dve_t, 1)
                    dve.wait_ge(dve_t, (it - 1) * DVE_T + count["t"])

                def statistics():
                    for i in range(NP):
                        last = V.bn_stats(stats[:, i, :], r[:, i, :])
                    step_t(last)
                    V.memset(rstd[:, :, :], 0.0)
                    for i in range(NP):
                        last = V.bn_aggr(mv[:, i, :], stats[:, i, :])
                    step_t(last)
                    V.tensor_scalar(rstd[:, 0, :], mv[:, :, 1], EPS, None, ALU.add).then_inc(ln_stats, 1)

                def normalise(which, dst, ready):
                    dve.wait_ge(rstd_ready, (it - 1) * 3 + which + 1)
                    for i in range(NP):
                        last = V.tensor_scalar(dst[:, i, :], r[:, i, :], mv[:, i, 0:1], rstd[:, 1, i:i + 1],
                                               ALU.subtract, ALU.mult)
                    last.then_inc(ready, 1)

                def convolve(c):
                    bank, _, read = numbers(f"raw{c}", it)
                    dve.wait_ge(bank_read[bank], read)
                    if c == 0:
                        wait(dve, th_ready, it)
                    y = batches(xc[:, c, :])
                    step_a(V.tensor_scalar(y, rawp[:, c, :, 0:S], conv_w[:, 0, c:c + 1], conv_b[:, c:c + 1],
                                           ALU.mult, ALU.add))
                    for k in range(1, KC):
                        ins = V.scalar_tensor_tensor(y, rawp[:, c, :, k:k + S], conv_w[:, k, c:c + 1], y,
                                                     ALU.mult, ALU.add)
                        if k < KC - 1:
                            step_a(ins)
                    ins.then_inc(xc_ready, 1)

                def softmax_shift(i):
                    dve.wait_ge(sc_ready, (it - 1) * NP + i + 1)
                    src = sc[i % 2].rearrange("p c (h s) -> p (c h) s", s=S)
                    if i >= 2:
                        dve.wait_ge(sm_ready, (it - 1) * NP + i - 1)
                    step_t(V.tensor_reduce(nmax[:, i % 2, :], src, AX.X, ALU.max, negate=True))
                    if i >= 2:
                        dve.wait_ge(pt_ready, (it - 1) * NP + i - 1)
                    V.tensor_tensor(pr[:, i % 2, :].rearrange("p (h s) -> p h s", s=S), src,
                                    nmax[:, i % 2, :].unsqueeze(2).to_broadcast([P, H, S]), ALU.add).then_inc(sm_ready, 1)

                def copy_probs(i):
                    dve.wait_ge(pt_ready, (it - 1) * NP + i + 1)
                    if i >= 2:
                        dve.wait_ge(work_ready, numbers(f"pv{i - 2}", it)[1])
                    V.tensor_copy(prT[:, i % 2, 4 * P:8 * P], ps[:, PT_BANK + 1, :]).then_inc(pt_dve, 1)

                def divide(i):
                    src, done = wait_ready(f"pv{i}", it)
                    heads = src[:, 0:H * VW].rearrange("p (h d) -> p h d", d=VW)
                    if i >= 2:
                        dve.wait_ge(done, numbers(f"pv{i - 2}", it)[2])
                    step_t(V.reciprocal(rden[:, i % 2, :], heads[:, :, HD]))
                    V.tensor_tensor(att[:, i, :].rearrange("p (h d) -> p h d", d=HD), heads[:, :, 0:HD],
                                    rden[:, i % 2, :].unsqueeze(2).to_broadcast([P, H, HD]), ALU.mult).then_inc(done, 1)

                if do_t:
                    src, done = wait_ready("outp", it)
                    dve.wait_ge(xres_loaded, it * 16)
                    V.tensor_tensor(r[:, :, :], src.rearrange("p (i d) -> p i d", i=NP), x_res[:, :, :],
                                    ALU.add).then_inc(done, 1)
                    dve.wait_ge(done, numbers("outp", it)[2])
                    statistics()
                if do_a:
                    convolve(0)
                if do_t:
                    normalise(0, x1, x1_ready)
                if do_a:
                    convolve(1)
                    for c in range(NH2):
                        dve.wait_ge(tg_ready, it * 2 + c + 1)
                        src, done = wait_ready(f"gate{c}", it)
                        V.scalar_tensor_tensor(sg[:, c, :], tg[:, c, :], 1.0, src, ALU.add, ALU.mult).then_inc(done, 1)
                    dve.wait_ge(th_ready, it + 1)
                    V.scalar_tensor_tensor(h[:, :, :], th[:, :, :], 1.0, xc[:, :, :], ALU.add,
                                           ALU.mult).then_inc(h_ready, 1)
                if do_t:
                    softmax_shift(0)
                if do_a:
                    bank, _, read = numbers("ssp", it)
                    dve.wait_ge(split_act, it * 3 + 1)
                    V.tensor_copy(rest[:, :], ssp[DTR:SSP, :]).then_inc(dve_a, 1)
                    count["a"] += 1
                    dve.wait_ge(dve_a, it * DVE_A + count["a"])
                    V.tensor_tensor(rest[:, :], rest[:, :], bc3[0:32, :], ALU.subtract).then_inc(split_dve, 1)
                if do_t:
                    softmax_shift(1)
                if do_a:
                    dve.wait_ge(split_act, it * 3 + 3)
                    V.tensor_tensor(bc3[64:96, :], rest[:, :], mid[:, :], ALU.subtract).then_inc(split_dve, 1)
                if do_a:
                    dve.wait_ge(bank_read[7], numbers("dt0", it)[2])
                    dve.wait_ge(bank_read[6], numbers("dt1", it)[2])
                    V.tensor_scalar(zr[:, :, :], z[:, :, :], 0.0, None, ALU.max).then_inc(zr_ready, 1)
                if do_t:
                    copy_probs(0)
                    for i in range(NP):
                        if i + 2 < NP:
                            softmax_shift(i + 2)
                        if i + 1 < NP:
                            copy_probs(i + 1)
                        divide(i)
                if do_a:
                    for i in range(2):
                        last = V.memset(da[i].rearrange("p c (b s) -> p (c b) s", s=S)[:, :, 0:1], 0.0)
                    last.then_inc(da_clear, 1)
                    src, done = wait_ready("v", it)
                    for e in range(2):
                        half = slice(e * S, (e + 1) * S)
                        last = V.tensor_tensor(
                            v_bd[half, :, :, e * VW:e * VW + HD],
                            src[half, :].rearrange("p (b c d) -> p b c d", b=NB, d=HD),
                            bv[half, :].rearrange("p (c e d) -> p c e d", e=2, d=HD)[:, :, e, :]
                            .unsqueeze(1).to_broadcast([S, NB, HP, HD]), ALU.add)
                    last.then_inc(done, 1)

                def tail(n):
                    if n == 6:
                        dve.wait_ge(bank_read[7], numbers("wo", it)[2])
                        dve.wait_ge(x1b_ready, it)
                        step_t(V.tensor_tensor(r[:, :, :], r2[:, :, :], x1b[:, :, :], ALU.add))
                        statistics()
                    if n == 7:
                        normalise(1, x2, x2_ready)
                    if n == 12:
                        dve.wait_ge(bank_read[7], numbers("ffn", it)[2])
                        V.tensor_tensor(f[:, :, :], f[:, :, :], bf[:, :].unsqueeze(1).to_broadcast([P, NP, D]),
                                        ALU.add).then_inc(fin_ready, 1)
                    if n == 14:
                        dve.wait_ge(f_ready, it)
                        step_t(V.tensor_tensor(r[:, :, :], x2[:, :, :], f[:, :, :], ALU.add))
                        statistics()
                    if n == 15:
                        dve.wait_ge(stored, it * 16)
                        normalise(2, o, o_ready)

                def scan(n):
                    dve.wait_ge(exp_ready, (it * NS + n + 1) * 2)
                    dve.wait_ge(dbu_ready, it * NS + n + 1)
                    if n >= 3:
                        dve.wait_ge(cs_ready, it * NS + n - 2)
                    V.tensor_tensor_scan(st[:, n % 3, :], da[n % 2].rearrange("p c r -> p (c r)"), dbu[:, n % 2, :],
                                         0.0, ALU.mult, ALU.add).then_inc(scanned, 1)

                if do_a:
                    scan(0)
                for n in range(NS):
                    if do_a and n + 1 < NS:
                        scan(n + 1)
                    if do_t:
                        tail(n)
                    if do_a:
                        dve.wait_ge(scanned, it * NS + n + 1)
                        dve.wait_ge(c_ready, it * NS + n + 1)
                        if n >= 2:
                            dve.wait_ge(y_added, it * NS + n - 1)
                        V.tensor_tensor(cs[:, n % 2, :].rearrange("p (c r) -> p c r", c=NH2),
                                        st[:, n % 3, :].rearrange("p (c r) -> p c r", c=NH2),
                                        ps[:, C_BANK, :].unsqueeze(1).to_broadcast([P, NH2, R]),
                                        ALU.mult).then_inc(cs_ready, 1)
                if do_a:
                    dve.wait_ge(y_added, (it + 1) * NS)
                    for c in range(NH2):
                        ins = V.scalar_tensor_tensor(st[:, 0, c * R:(c + 1) * R], h[:, c, :], d_skip[:, c:c + 1],
                                                     ps[:, Y_BANK + c, :], ALU.mult, ALU.add)
                    step_a(ins)
                    V.tensor_tensor(yg[:, :, :], st[:, 0, :].rearrange("p (c r) -> p c r", c=NH2), sg[:, :, :],
                                    ALU.mult).then_inc(yg_ready, 1)
                assert not do_a or count["a"] == DVE_A, count
                assert not do_t or count["t"] == DVE_T, count

            over_groups(dve, iteration)

        @block.gpsimd
        def _(pool):
            Q = nc.gpsimd
            Q.memset(ident[:, :], 0.0).then_inc(pool_const, 1)
            Q.memset(k_bd[:, :, :, :], 0.0).then_inc(pool_const, 1)
            Q.memset(v_bd[:, :, :, :], 0.0).then_inc(pool_const, 1)
            Q.memset(rawp[:, :, :, :], 0.0).then_inc(pool_const, 1)
            Q.memset(mhalf[:, :], -0.5).then_inc(pool_const, 1)
            pool.wait_ge(pool_const, 5)
            Q.affine_select(out=ident[:, :], in_=ident[:, :], compare_op=ALU.not_equal, fill=1.0, base=0,
                            pattern=[[-1, P]], channel_multiplier=1).then_inc(pool_const, 1)
            pool.wait_ge(pool_const, POOL_CONSTS)
            pool.wait_ge(consts_in, N_CONSTS * 16)

            def iteration(it, do_a, do_t):
                def inverse_deviation(which):
                    pool.wait_ge(ln_stats, (it - 1) * 3 + which + 1)
                    Q.tensor_tensor(rstd[:, 1, :], rstd[:, 0, :], mhalf[:, :], ALU.pow).then_inc(rstd_ready, 1)

                if do_t:
                    inverse_deviation(0)
                    pool.wait_ge(x1_ready, it)
                    Q.tensor_tensor(x1b[:, :, :], x1[:, :, :], bo[:, :].unsqueeze(1).to_broadcast([P, NP, D]),
                                    ALU.add).then_inc(x1b_ready, 1)
                if do_a:
                    pool.wait_ge(sp_step, it * 3 + 3)
                    pool.wait_ge(zr_ready, it + 1)
                    Q.tensor_tensor(dt[:, :, :], zr[:, :, :], az[:, :, :], ALU.add).then_inc(dt_ready, 1)
                    pool.wait_ge(dt_ready, it + 1)
                    pool.wait_ge(h_ready, it + 1)
                    Q.tensor_tensor(u[:, :, :], dt[:, :, :], h[:, :, :], ALU.mult).then_inc(u_ready, 1)
                    pool.wait_ge(u_ready, it + 1)
                for n in range(NS):
                    if do_a:
                        pool.wait_ge(bank_read[7], numbers(f"B{n}", it)[2])
                        if n >= 2:
                            pool.wait_ge(scanned, it * NS + n - 1)
                        Q.tensor_tensor(dbu[:, n % 2, :].rearrange("p (c r) -> p c r", c=NH2), u[:, :, :],
                                        b_all[:, n % (AHEAD + 1), :].unsqueeze(1).to_broadcast([P, NH2, R]),
                                        ALU.mult).then_inc(dbu_ready, 1)
                    if do_t and n == 7:
                        inverse_deviation(1)
                    if do_t and n == NS - 1:
                        inverse_deviation(2)

            over_groups(pool, iteration)


N_CONSTS = 26
POOL_CONSTS = 6
ACT_CONSTS = 7
DVE_CONSTS = 11
DVE_A = 8
DVE_T = 16


_INS = ["x", "ctx_1024", "mask_1x1xSxS2_ik0", "L0_attn_W_in", "L0_attn_conv_w", "L0_attn_conv_b", "L0_attn_W_x",
        "L0_attn_W_dt", "L0_attn_b_dt", "L0_attn_A_log", "L0_attn_D", "L0_attn_W_out", "L0_xattn_Wq",
        "L0_xattn_bq", "L0_xattn_Wk", "L0_xattn_bk", "L0_xattn_Wv", "L0_xattn_bv", "L0_xattn_Wo", "L0_xattn_bo",
        "L0_ffn_weight", "L0_ffn_aux_weight1", "L0_ffn_aux_weight2", "L0_ffn_bias"]


def kernel(**inputs):
    import numpy as _np
    import concourse.bacc as _bacc
    from concourse import mybir as _mybir
    from concourse.bass_utils import run_bass_kernel_spmd as _run

    nc = _bacc.Bacc("TRN2", target_bir_lowering=False, num_devices=1)
    arrays, args = {}, {}
    for name in _INS:
        a = _np.ascontiguousarray(inputs[name])
        arrays[f"in_{name}_dram"] = a
        args[name] = nc.dram_tensor(f"in_{name}_dram", a.shape, _mybir.dt.from_np(a.dtype), kind="ExternalInput").ap()
    out = nc.dram_tensor("out_0_dram", inputs["x"].shape, _mybir.dt.float32, kind="ExternalOutput").ap()
    decoder_layer(nc, args, out)
    r = _run(nc, [arrays], core_ids=[0])
    return r.results[0]["out_0_dram"]
```

```python
import numpy as np
import concourse.bass as bass
from concourse import mybir
from contextlib import ExitStack


def decoder_layer(nc, t, out_dram):
    F32, BF16, I32 = mybir.dt.float32, mybir.dt.bfloat16, mybir.dt.int32
    ALU, ACT, AX = mybir.AluOpType, mybir.ActivationFunctionType, mybir.AxisListType

    B, S, D = t["x"].shape
    P = 128
    NB = 8
    R = NB * S
    G = B // NB
    NP = R // P
    CH = t["L0_attn_W_out"].shape[0]
    NH2 = CH // P
    NS = t["L0_attn_A_log"].shape[1]
    KC = t["L0_attn_conv_w"].shape[0]
    DTR = t["L0_attn_W_dt"].shape[0]
    SSP = DTR + 2 * NS
    H = 16
    HD = D // H
    HP = H // 2
    NU = 2 * NP
    SP_ = KC - 1 + S
    VW = HD + 1
    EPS = 1e-5
    NEG = -1.0e30
    QSCALE = float(HD) ** -0.5
    assert R == 512 and NH2 == 2 and NP == 4 and SSP == 96 and SSP - DTR == 32 and NS == 16 and G % 2 == 0

    DA_BANK, C_BANK, Y_BANK = 0, 2, 3
    PIECES = [
        [("xtr", 7, "A"), ("atr", 5, "U"), ("outp", 6, "T")],
        [("raw0", 7, "A"), ("wo", 6, "U")],
        [("raw1", 7, "A"), ("x1tr", 5, "T")],
        [("qT", 7, "T"), ("x2tr", 5, "U")],
        [("sc0", 6, "T"), ("ffn", 7, "U")],
        [("sc1", 6, "T"), ("ctr", 7, "S")],
        [("sc2", 6, "T"), ("pt0", 7, "T")],
        [("sc3", 6, "T"), ("pt1", 7, "T"), ("ssp", 5, "A")],
        [("sc4", 6, "T"), ("pt2", 7, "T"), ("pv0", 5, "T")],
        [("sc5", 6, "T"), ("pt3", 7, "T"), ("dt0", 5, "A")],
        [("sc6", 6, "T"), ("pt4", 7, "T"), ("pv1", 5, "T")],
        [("sc7", 6, "T"), ("pt5", 7, "T"), ("dt1", 5, "A")],
        [("pt6", 7, "T"), ("pv2", 5, "T"), ("kT", 6, "S")],
        [("pt7", 7, "T"), ("gate0", 6, "A")],
        [("gate1", 7, "A"), ("pv3", 5, "T")],
        [("v", 6, "S")]]
    JOBS = []
    for n in range(NS):
        JOBS.append((f"B{(n + 2) % NS}", 5, "S" if n + 2 < NS else "A"))
        JOBS += PIECES[n]

    def kinds(k):
        if not isinstance(k, int):
            return "SATU"
        return "".join(c for c, first in (("A", -1), ("S", 0), ("T", 1), ("U", 2)) if first <= k < first + G)

    def jobs(k, bank=None):
        return [j for j in JOBS if j[2] in kinds(k) and bank in (None, j[1])]

    def before(k, bank=None):
        if isinstance(k, int):
            return sum(len(jobs(i, bank)) for i in range(-1, k))
        return (k - 2) * len(jobs(2, bank)) + before(2, bank)

    def bank_of(name):
        return next(j[1] for j in JOBS if j[0] == name)

    def ready(name, k):
        return before(k) + [j[0] for j in jobs(k)].index(name) + 1

    def read(name, k):
        bank = bank_of(name)
        return before(k, bank) + [j[0] for j in jobs(k, bank)].index(name) + 1

    def ready_b1(k):
        return before(k) - ("S" in kinds(k - 1))

    def read_b(j, k):
        return read(f"B{j}", k) if j > 1 else before(k, 5)

    def wait(eng, semaphore, value):
        if not (isinstance(value, int) and value <= 0):
            eng.wait_ge(semaphore, value)

    ctx = ExitStack()
    with ctx:
        def sb(name, shape, dt=F32):
            return ctx.enter_context(nc.sbuf_tensor(name, shape, dt))

        def sem(name):
            return ctx.enter_context(nc.semaphore(name))

        ident = sb("ident", [P, P])
        identb = sb("identb", [P, P], BF16)
        sel = sb("sel", [SSP, 2 * NS, P], BF16)
        mhalf = sb("mhalf", [P, NP])
        maski = sb("maski", [P, S], I32)
        maskneg = sb("maskneg", [P, S], BF16)
        w_in = sb("w_in", [P, 2 * CH])
        conv_w = sb("conv_w", [P, KC, NH2])
        conv_b = sb("conv_b", [P, NH2])
        w_x = sb("w_x", [P, NH2, SSP])
        w_dt = sb("w_dt", [SSP, CH])
        b_dt = sb("b_dt", [P, NH2])
        a_neg = sb("a_neg", [P, NH2, NS])
        d_skip = sb("d_skip", [P, NH2])
        w_out = sb("w_out", [P, NH2, D])
        wraw = sb("wraw", [P, 7, D])
        wT = sb("wT", [P, 6, D])
        w_ffn = sb("w_ffn", [P, 2, D])
        bq = sb("bq", [P, 1])
        bk = sb("bk", [P, 1])
        bv = sb("bv", [P, D])
        bo = sb("bo", [P, D])
        bf = sb("bf", [P, D])
        x_in = sb("x_in", [P, NP, D])
        ctx_in = sb("ctx_in", [P, NP, D])
        xT = sb("xT", [P, R])
        ctxT = sb("ctxT", [P, R])
        kT = sb("kT", [P, NB, S])
        k_bd = sb("k_bd", [P, NB, H, S])
        v_bd = sb("v_bd", [P, NB, HP, 2 * VW])
        rawp = sb("rawp", [P, NH2, NB, SP_])
        xc = sb("xc", [P, NH2, R])
        th = sb("th", [P, NH2, R])
        h = sb("h", [P, 2, NH2, R])
        sg = sb("sg", [P, 2, NH2, R])
        ssp = sb("ssp", [SSP, R])
        bc3 = sb("bc3", [SSP, 2, R], BF16)
        rest = sb("rest", [32, R])
        mid = sb("mid", [32, R], BF16)
        z = sb("z", [P, NH2, R])
        dt = sb("dt", [P, 2, NH2, R])
        u = sb("u", [P, NH2, R])
        b_all = sb("b_all", [P, 4, R])
        dbu = sb("dbu", [P, 2, NH2 * R])
        st = sb("st", [P, 2, NH2 * R])
        cs = sb("cs", [P, 2, NH2 * R])
        yg = sb("yg", [P, NH2, R])
        x_res = sb("x_res", [P, NP, D])
        r = sb("r", [P, 2, NP, D])
        stats = sb("stats", [P, NP, 6])
        mv = sb("mv", [P, 3, NP, 2])
        rstd = sb("rstd", [P, 3, 2, NP])
        x1 = sb("x1", [P, NP, D])
        x1b = sb("x1b", [P, NP, D])
        x1T = sb("x1T", [P, R])
        qT = sb("qT", [P, R])
        nmax = sb("nmax", [P, 2, H // 2])
        pr = sb("pr", [P, 3, R])
        prT = sb("prT", [P, 3, R])
        rden = sb("rden", [P, 2, H])
        att = sb("att", [P, NP, D])
        attT = sb("attT", [P, R])
        x2 = sb("x2", [P, NP, D])
        x2T = sb("x2T", [P, R])
        f = sb("f", [P, NP, D])
        o = sb("o", [P, NP, D])
        ps = ctx.enter_context(nc.psum_tensor("ps", [P, 8, 512], F32))
        da = ps[:, DA_BANK:DA_BANK + 2, :]

        consts_in = sem("consts_in")
        x_loaded, ctx_loaded, xres_loaded = sem("x_loaded"), sem("ctx_loaded"), sem("xres_loaded")
        kbd_loaded = sem("kbd_loaded")
        stored = sem("stored")
        pool_const, act_const, dve_const, pe_const = (sem("pool_const"), sem("act_const"), sem("dve_const"),
                                                      sem("pe_const"))
        work_ready = sem("work_ready")
        c_ready = sem("c_ready")
        y_added = sem("y_added")
        bank_read = {5: sem("bank5_read"), 6: sem("bank6_read"), 7: sem("bank7_read")}
        tap_ready = sem("tap_ready")
        th_ready = sem("th_ready")
        tg_ready = sem("tg_ready")
        sp_step = sem("sp_step")
        split_act = sem("split_act")
        exp_ready = sem("exp_ready")
        pr_ready = sem("pr_ready")
        f_ready = sem("f_ready")
        dve_a, dve_t, dve_u = sem("dve_a"), sem("dve_t"), sem("dve_u")
        xc_ready = sem("xc_ready")
        h_ready = sem("h_ready")
        split_dve = sem("split_dve")
        scanned = sem("scanned")
        cs_ready = sem("cs_ready")
        yg_ready = sem("yg_ready")
        ln_stats = [sem(f"ln{i}_stats") for i in range(3)]
        x1_ready, x2_ready, o_ready = sem("x1_ready"), sem("x2_ready"), sem("o_ready")
        zr_ready = sem("zr_ready")
        dt_ready = sem("dt_ready")
        u_ready = sem("u_ready")
        dbu_ready = sem("dbu_ready")
        rstd_ready = [sem(f"ln{i}_rstd") for i in range(3)]
        x1b_ready = sem("x1b_ready")

        x_rows = t["x"].rearrange("(g i b) s d -> g (b s) i d", g=G, i=NP)
        ctx_rows = t["ctx_1024"].rearrange("(g i b) s d -> g (b s) i d", g=G, i=NP)
        out_rows = out_dram.rearrange("(g i b) s d -> g (b s) i d", g=G, i=NP)

        def over_groups(eng, iteration):
            for k in (-1, 0, 1):
                iteration(k, k % 2)
            with eng.Fori(2, G - 3, 2) as k:
                iteration(k, 0)
                iteration(k + 1, 1)
            for k in range(G - 2, G + 2):
                iteration(k, k % 2)

        block = ctx.enter_context(nc.Block())

        @block.sync
        def _(sp):
            col = lambda a: a.rearrange("(p o) -> p o", o=1)
            row = lambda a: a.rearrange("(o n) -> o n", o=1).to_broadcast([P, D])
            loads = [(w_in[:, :], t["L0_attn_W_in"]),
                     (w_x[:, :, :], t["L0_attn_W_x"].rearrange("(c p) n -> p c n", p=P)),
                     (w_dt[0:DTR, :], t["L0_attn_W_dt"]),
                     (conv_b[:, :], t["L0_attn_conv_b"].rearrange("(c p) -> p c", p=P)),
                     (b_dt[:, :], t["L0_attn_b_dt"].rearrange("(c p) -> p c", p=P)),
                     (d_skip[:, :], t["L0_attn_D"].rearrange("(c p) -> p c", p=P)),
                     (a_neg[:, :, :], t["L0_attn_A_log"].rearrange("(c p) n -> p c n", p=P)),
                     (w_out[:, :, :], t["L0_attn_W_out"].rearrange("(c p) n -> p c n", p=P)),
                     (bq[:, :], col(t["L0_xattn_bq"])), (bk[:, :], col(t["L0_xattn_bk"])),
                     (bv[:, :], row(t["L0_xattn_bv"])), (bo[:, :], row(t["L0_xattn_bo"])),
                     (bf[:, :], row(t["L0_ffn_bias"])),
                     (maski[0:S, :], t["mask_1x1xSxS2_ik0"][0, 0]),
                     (maski[S:2 * S, :], t["mask_1x1xSxS2_ik0"][0, 0])]
            loads += [(conv_w[:, k, :], t["L0_attn_conv_w"][k, 0].rearrange("(c p) -> p c", p=P)) for k in range(KC)]
            loads += [(wraw[:, i, :], t[n]) for i, n in enumerate(
                ("L0_xattn_Wq", "L0_xattn_Wk", "L0_xattn_Wv", "L0_xattn_Wo",
                 "L0_ffn_weight", "L0_ffn_aux_weight1", "L0_ffn_aux_weight2"))]
            assert len(loads) == N_CONSTS
            sp.dma_start(x_in[:, :, :], x_rows[0]).then_inc(x_loaded, 16)
            sp.dma_start(ctx_in[:, :, :], ctx_rows[0]).then_inc(ctx_loaded, 16)
            with nc.allow_non_contiguous_dma(reason="channels of small vectors go to the partitions"):
                for dst, src in loads:
                    sp.dma_start(dst, src).then_inc(consts_in, 16)

            def iteration(k, par):
                kk = kinds(k)
                static = isinstance(k, int)
                if "A" in kk and not (static and k + 2 >= G):
                    sp.wait_ge(bank_read[7], read("xtr", k))
                    sp.dma_start(x_in[:, :, :], x_rows[k + 2]).then_inc(x_loaded, 16)
                if "S" in kk:
                    if "T" in kk:
                        sp.wait_ge(bank_read[6], read("outp", k))
                    sp.dma_start(x_res[:, :, :], x_rows[k]).then_inc(xres_loaded, 16)
                if "S" in kk and not (static and k + 1 >= G):
                    sp.wait_ge(bank_read[7], read("ctr", k))
                    sp.dma_start(ctx_in[:, :, :], ctx_rows[k + 1]).then_inc(ctx_loaded, 16)
                if "U" in kk:
                    sp.wait_ge(o_ready, k - 1)
                    sp.dma_start(out_rows[k - 2], o[:, :, :]).then_inc(stored, 16)
                if "S" in kk:
                    sp.wait_ge(bank_read[6], read("kT", k))
                    if static and k == 0:
                        sp.wait_ge(pool_const, POOL_CONSTS)
                    for hh in range(H):
                        sp.dma_start(k_bd[hh * HD:(hh + 1) * HD, :, hh, :],
                                     kT[hh * HD:(hh + 1) * HD, :, :]).then_inc(kbd_loaded, 16)

            over_groups(sp, iteration)
            sp.wait_ge(stored, (G + 1) * 16)

        @block.tensor
        def _(pe):
            mm = nc.tensor.matmul

            pe.wait_ge(consts_in, N_CONSTS * 16)
            pe.wait_ge(pool_const, POOL_CONSTS)
            for i in range(6):
                last = nc.tensor.transpose(ps[:, 4 + i // 4, (i % 4) * P:(i % 4 + 1) * P], wraw[:, i, :], ident[:, :])
            last.then_inc(pe_const, 1)
            pe.wait_ge(act_const, 3)
            mm(ps[:, 6, 0:D], wT[:, 5, :], wraw[:, 6, :], start=True, stop=True).then_inc(pe_const, 1)
            pe.wait_ge(act_const, 4)
            mm(ps[:, 7, 0:D], wT[:, 4, :], w_ffn[:, 0, :], start=True, stop=True).then_inc(pe_const, 1)
            pe.wait_ge(act_const, ACT_CONSTS)
            pe.wait_ge(dve_const, DVE_CONSTS)

            def iteration(k, par):
                kk = kinds(k)
                nxt = 1 - par

                def job(name):
                    wait(pe, bank_read[bank_of(name)], read(name, k) - 1)
                    return ps[:, bank_of(name), :]

                def wait_read(name):
                    pe.wait_ge(bank_read[bank_of(name)], read(name, k))

                def transposes(bank, src):
                    for i in range(NP):
                        last = nc.tensor.transpose(bank[:, i * P:(i + 1) * P], src[:, i, :], ident[:, :])
                    last.then_inc(work_ready, 1)

                def rows_times(bank, lhsT, weights):
                    for i in range(NP):
                        last = mm(bank[:, i * D:(i + 1) * D], lhsT[:, i * P:(i + 1) * P], weights,
                                  start=True, stop=True)
                    last.then_inc(work_ready, 1)

                def scores(j):
                    i, c = j // 2, j % 2
                    bank = job(f"sc{j}")
                    if j == 0:
                        wait_read("qT")
                        pe.wait_ge(kbd_loaded, k * H * 16)
                    mm(bank, identb[:, :], maskneg[:, :].unsqueeze(1).to_broadcast([P, H // 2, S]),
                       start=True, stop=False, skip_group_check=True)
                    for b in range(2):
                        last = mm(bank[b * S:(b + 1) * S, :], qT[:, (2 * i + b) * S:(2 * i + b + 1) * S],
                                  k_bd[:, 2 * i + b, c * H // 2:(c + 1) * H // 2, :],
                                  start=False, stop=True, skip_group_check=True)
                    last.then_inc(work_ready, 1)

                def transpose_probs(j):
                    bank = job(f"pt{j}")
                    pe.wait_ge(pr_ready, (k - 1) * NU + j + 1)
                    for c in range(HP // 2):
                        last = nc.tensor.transpose(bank[:, c * P:(c + 1) * P], pr[:, j % 3, c * P:(c + 1) * P],
                                                   ident[:, :])
                    last.then_inc(work_ready, 1)

                def weigh_values(i):
                    bank = job(f"pv{i}")
                    wait_read(f"pt{2 * i + 1}")
                    for c in range(HP):
                        src = prT[:, (2 * i + c // 4) % 3, :]
                        for b in range(2):
                            last = mm(bank[b * S:(b + 1) * S, c * 2 * VW:(c + 1) * 2 * VW],
                                      src[:, (c % 4) * P + b * S:(c % 4) * P + (b + 1) * S],
                                      v_bd[:, 2 * i + b, c, :], start=True, stop=True, skip_group_check=True)
                    last.then_inc(work_ready, 1)

                def add_y(n):
                    for c in range(NH2):
                        last = mm(ps[:, Y_BANK + c, :], ident[:, :], cs[:, n % 2, c * R:(c + 1) * R],
                                  start=n == 0, stop=n == NS - 1, skip_group_check=True)
                    last.then_inc(y_added, 1)

                def piece(name):
                    kind, c = (name[:-1], int(name[-1])) if name[-1].isdigit() else (name, 0)
                    if kind == "xtr":
                        pe.wait_ge(x_loaded, (k + 2) * 16)
                        transposes(job(name), x_in)
                    if kind == "raw":
                        bank = job(name)
                        wait_read("xtr")
                        mm(bank, w_in[:, c * P:(c + 1) * P], xT[:, :], start=True, stop=True).then_inc(work_ready, 1)
                    if kind == "gate":
                        mm(job(name), w_in[:, CH + c * P:CH + (c + 1) * P], xT[:, :],
                           start=True, stop=True).then_inc(work_ready, 1)
                    if kind == "ssp":
                        bank = job(name)
                        pe.wait_ge(h_ready, k + 2)
                        for c in range(NH2):
                            last = mm(bank[0:SSP, :], w_x[:, c, :], h[:, nxt, c, :], start=c == 0, stop=c == NH2 - 1)
                        last.then_inc(work_ready, 1)
                    if kind == "dt":
                        bank = job(name)
                        wait_read("ssp")
                        mm(bank, w_dt[:, c * P:(c + 1) * P], ssp[:, :], start=True, stop=True).then_inc(work_ready, 1)
                    if kind == "ctr":
                        pe.wait_ge(ctx_loaded, (k + 1) * 16)
                        transposes(job(name), ctx_in)
                    if kind == "kT":
                        bank = job(name)
                        wait_read("ctr")
                        mm(bank, wT[:, 1, :], ctxT[:, :], start=True, stop=True).then_inc(work_ready, 1)
                    if kind == "v":
                        bank = job(name)
                        for b in range(NB):
                            for e in range(2):
                                last = mm(bank[e * S:(e + 1) * S, b * HP * HD:(b + 1) * HP * HD],
                                          ctxT[:, b * S:(b + 1) * S],
                                          wT[:, 2, :].rearrange("p (c e d) -> p c e d", e=2, d=HD)[:, :, e, :],
                                          start=True, stop=True, skip_group_check=True)
                        last.then_inc(work_ready, 1)
                    if kind == "outp":
                        bank = job(name)
                        pe.wait_ge(yg_ready, k)
                        for i in range(NP):
                            for c in range(NH2):
                                last = mm(bank[:, i * D:(i + 1) * D], yg[:, c, i * P:(i + 1) * P], w_out[:, c, :],
                                          start=c == 0, stop=c == NH2 - 1)
                        last.then_inc(work_ready, 1)
                    if kind == "x1tr":
                        bank = job(name)
                        pe.wait_ge(x1_ready, k)
                        transposes(bank, x1)
                    if kind == "qT":
                        bank = job(name)
                        wait_read("x1tr")
                        mm(bank, wT[:, 0, :], x1T[:, :], start=True, stop=True).then_inc(work_ready, 1)
                    if kind == "sc":
                        scores(c)
                    if kind == "pt":
                        transpose_probs(c)
                    if kind == "pv":
                        weigh_values(c)
                    if kind == "atr":
                        transposes(job(name), att)
                    if kind == "wo":
                        bank = job(name)
                        wait_read("atr")
                        rows_times(bank, attT, wT[:, 3, :])
                    if kind == "x2tr":
                        bank = job(name)
                        pe.wait_ge(x2_ready, k - 1)
                        transposes(bank, x2)
                    if kind == "ffn":
                        bank = job(name)
                        wait_read("x2tr")
                        rows_times(bank, x2T, w_ffn[:, 1, :])

                for n in range(NS):
                    if "S" in kk:
                        wait(pe, cs_ready, k * NS + n)
                        mm(ps[:, C_BANK, :], sel[:, NS + n, :], bc3[:, par, :], start=True,
                           stop=True).then_inc(c_ready, 1)
                        if n == 1:
                            wait(pe, yg_ready, k)
                        if n > 0:
                            add_y(n - 1)
                        if n + 2 < NS:
                            mm(job(f"B{n + 2}"), sel[:, n + 2, :], bc3[:, par, :], start=True,
                               stop=True).then_inc(work_ready, 1)
                    if "A" in kk and n + 2 >= NS:
                        if n + 2 == NS:
                            pe.wait_ge(split_act, (k + 2) * 3)
                            pe.wait_ge(split_dve, (k + 2) * 2)
                        mm(job(f"B{n + 2 - NS}"), sel[:, n + 2 - NS, :], bc3[:, nxt, :], start=True,
                           stop=True).then_inc(work_ready, 1)
                    for name, _, kind in PIECES[n]:
                        if kind in kk:
                            piece(name)
                if "S" in kk:
                    pe.wait_ge(cs_ready, (k + 1) * NS)
                    add_y(NS - 1)

            over_groups(pe, iteration)

        @block.scalar
        def _(act):
            A = nc.scalar.activation

            act.wait_ge(consts_in, N_CONSTS * 16)
            A(a_neg[:, :, :], a_neg[:, :, :], ACT.Exp).then_inc(act_const, 1)
            act.wait_ge(pe_const, 1)
            A(wT[:, 0:4, :], ps[:, 4, :].rearrange("p (i d) -> p i d", i=4), ACT.Copy).then_inc(act_const, 1)
            A(wT[:, 4:6, :], ps[:, 5, 0:2 * D].rearrange("p (i d) -> p i d", i=2), ACT.Copy).then_inc(act_const, 1)
            act.wait_ge(pe_const, 2)
            A(w_ffn[:, 0, :], ps[:, 6, 0:D], ACT.Copy).then_inc(act_const, 1)
            act.wait_ge(pe_const, 3)
            A(w_ffn[:, 1, :], ps[:, 7, 0:D], ACT.Copy).then_inc(act_const, 1)
            A(w_in[:, CH:2 * CH], w_in[:, CH:2 * CH], ACT.Copy, scale=0.5).then_inc(act_const, 1)
            A(bq[:, :], bq[:, :], ACT.Copy, scale=QSCALE).then_inc(act_const, 1)
            act.wait_ge(act_const, ACT_CONSTS)
            act.wait_ge(dve_const, DVE_CONSTS)
            act.wait_ge(pool_const, POOL_CONSTS)

            def batches(ap):
                return ap.rearrange("p (b s) -> p b s", b=NB)

            def iteration(k, par):
                kk = kinds(k)
                nxt = 1 - par

                def work(name):
                    act.wait_ge(work_ready, ready(name, k))
                    return ps[:, bank_of(name), :]

                def copy(name, dst, func=ACT.Copy, **kw):
                    src = work(name)
                    if len(dst.shape) == 3:
                        src = src.rearrange("p (i d) -> p i d", i=dst.shape[1])
                    A(dst, src, func, **kw).then_inc(bank_read[bank_of(name)], 1)

                def exp_da(n):
                    if n == 0:
                        act.wait_ge(dt_ready, k + 1)
                    wait(act, scanned, k * NS + n)
                    for c in range(NH2):
                        A(batches(da[:, c, :])[:, :, 1:], batches(dt[:, par, c, :])[:, :, 1:], ACT.Exp,
                          scale=a_neg[:, c, n:n + 1]).then_inc(exp_ready, 1)

                def copy_b(j, group):
                    wait(act, dbu_ready, group * NS + j - 3)
                    if j == 1:
                        act.wait_ge(work_ready, ready_b1(k))
                    else:
                        act.wait_ge(work_ready, ready(f"B{j}", k))
                    A(b_all[:, j % 4, :], ps[:, 5, :], ACT.Copy).then_inc(bank_read[5], 1)

                def first_tap(c):
                    act.wait_ge(bank_read[7], read(f"raw{c}", k))
                    if c == 0:
                        wait(act, h_ready, k + 1)
                    A(batches(xc[:, c, :]), rawp[:, c, :, 0:S], ACT.Identity, bias=conv_b[:, c:c + 1],
                      scale=conv_w[:, 0, c:c + 1]).then_inc(tap_ready, 1)

                def pieces_a(m):
                    if m == 1:
                        copy("xtr", xT[:, :])
                    if m in (2, 3):
                        c = m - 2
                        copy(f"raw{c}", rawp[:, c, :, KC - 1:])
                    if m in (3, 4):
                        first_tap(m - 3)
                    if m == 6:
                        act.wait_ge(xc_ready, (k + 2) * 2)
                        A(th[:, :, :], xc[:, :, :], ACT.Tanh).then_inc(th_ready, 1)
                    if m == 8:
                        act.wait_ge(work_ready, ready("ssp", k))
                        A(ssp[:, :], ps[0:SSP, 5, :], ACT.Copy).then_inc(bank_read[5], 1)
                        act.wait_ge(bank_read[5], read("ssp", k))
                        A(bc3[0:32, nxt, :], ssp[DTR:SSP, :], ACT.Copy).then_inc(split_act, 1)
                    if m == 10:
                        copy("dt0", z[:, 0, :], ACT.Identity, bias=b_dt[:, 0:1])
                        act.wait_ge(split_dve, (k + 1) * 2 + 1)
                        A(mid[:, :], rest[:, :], ACT.Copy).then_inc(split_act, 1)
                        A(bc3[32:64, nxt, :], rest[:, :], ACT.Copy).then_inc(split_act, 1)
                    if m == 12:
                        copy("dt1", z[:, 1, :], ACT.Identity, bias=b_dt[:, 1:2])
                    if m == 13:
                        act.wait_ge(bank_read[5], read("dt1", k))
                        wait(act, exp_ready, k * NS * 2)
                        A(dt[:, nxt, :, :], z[:, :, :], ACT.Abs).then_inc(sp_step, 1)
                        act.wait_ge(sp_step, (k + 1) * 3 + 1)
                        A(dt[:, nxt, :, :], dt[:, nxt, :, :], ACT.Exp, scale=-1.0).then_inc(sp_step, 1)
                    if m == 14:
                        act.wait_ge(sp_step, (k + 1) * 3 + 2)
                        A(dt[:, nxt, :, :], dt[:, nxt, :, :], ACT.Ln, bias=1.0).then_inc(sp_step, 1)
                    if m in (14, 15):
                        c = m - 14
                        src = work(f"gate{c}")
                        A(th[:, c, :], src, ACT.Tanh).then_inc(tg_ready, 1)

                def pieces_s(m):
                    if m == 6:
                        copy("ctr", ctxT[:, :])
                    if m == 13:
                        wait(act, kbd_loaded, k * H * 16)
                        copy("kT", kT[:, :, :], ACT.Identity, bias=bk[:, 0:1])

                def pieces_t(m):
                    if m == 3:
                        copy("x1tr", x1T[:, :])
                    if m == 4:
                        copy("qT", qT[:, :], ACT.Identity, bias=bq[:, 0:1], scale=QSCALE)
                    if 6 <= m < 6 + NU:
                        j = m - 6
                        act.wait_ge(bank_read[6], read(f"sc{j}", k))
                        A(pr[:, j % 3, :], pr[:, j % 3, :], ACT.Exp).then_inc(pr_ready, 1)
                    if 7 <= m < 7 + NU:
                        j = m - 7
                        if j >= 3:
                            act.wait_ge(work_ready, ready(f"pv{(j - 3) // 2}", k))
                        copy(f"pt{j}", prT[:, j % 3, :])

                def pieces_u(m):
                    if m == 1:
                        copy("atr", attT[:, :])
                    if m == 4:
                        copy("x2tr", x2T[:, :])
                    if m == 12:
                        act.wait_ge(bank_read[7], read("ffn", k))
                        A(f[:, :, :], f[:, :, :], ACT.Tanh).then_inc(f_ready, 1)

                for m in range(NS):
                    if "S" in kk:
                        exp_da(m)
                        if m + 1 < NS:
                            copy_b(m + 1, k)
                    if "A" in kk and m + 1 == NS:
                        copy_b(0, k + 1)
                    if "A" in kk:
                        pieces_a(m)
                    if "T" in kk:
                        pieces_t(m)
                    if "U" in kk:
                        pieces_u(m)
                    if "S" in kk:
                        pieces_s(m)

            over_groups(act, iteration)

        @block.vector
        def _(dve):
            V = nc.vector
            count = {}

            dve.wait_ge(consts_in, N_CONSTS * 16)
            V.tensor_scalar(maskneg[:, :], maski[:, :], 0, NEG, ALU.is_equal, ALU.mult).then_inc(dve_const, 1)
            V.tensor_scalar(conv_w[:, :, :], conv_w[:, :, :], 0.5, None, ALU.mult).then_inc(dve_const, 1)
            V.tensor_scalar(conv_b[:, :], conv_b[:, :], 0.5, None, ALU.mult).then_inc(dve_const, 1)
            V.memset(da, 0.0).then_inc(dve_const, 1)
            dve.wait_ge(act_const, ACT_CONSTS)
            V.tensor_scalar(a_neg[:, :, :], a_neg[:, :, :], -1.0, None, ALU.mult).then_inc(dve_const, 1)
            dve.wait_ge(pool_const, POOL_CONSTS)
            V.tensor_copy(identb[:, :], ident[:, :]).then_inc(dve_const, 1)
            V.memset(o[:, :, :], 0.0).then_inc(stored, 16)
            V.memset(w_dt[DTR:SSP, :], 0.0).then_inc(dve_const, 1)
            for e in range(2):
                V.memset(v_bd[e * S:(e + 1) * S, :, :, e * VW + HD:e * VW + HD + 1], 1.0).then_inc(dve_const, 1)
            for j in range(3):
                V.tensor_copy(sel[32 * j:32 * j + 32, :, :],
                              ident[32 * j:32 * j + 32, 32 * j:32 * j + 32].unsqueeze(2)
                              .to_broadcast([32, 32, P])).then_inc(dve_const, 1)
            dve.wait_ge(dve_const, DVE_CONSTS)

            def batches(ap):
                return ap.rearrange("p (b s) -> p b s", b=NB)

            def iteration(k, par):
                kk = kinds(k)
                nxt = 1 - par
                count["a"] = count["t"] = count["u"] = 0

                def step_a(ins):
                    count["a"] += 1
                    ins.then_inc(dve_a, 1)
                    dve.wait_ge(dve_a, (k + 1) * DVE_A + count["a"])

                def step_t(ins):
                    count["t"] += 1
                    ins.then_inc(dve_t, 1)
                    dve.wait_ge(dve_t, (k - 1) * DVE_T + count["t"])

                def step_u(ins):
                    count["u"] += 1
                    ins.then_inc(dve_u, 1)
                    dve.wait_ge(dve_u, (k - 2) * DVE_U + count["u"])

                def work(name):
                    dve.wait_ge(work_ready, ready(name, k))
                    return ps[:, bank_of(name), :]

                def rows(bank):
                    return bank.rearrange("p (i d) -> p i d", i=NP)

                def statistics(w, step):
                    for i in range(NP):
                        last = V.bn_stats(stats[:, i, :], r[:, w % 2, i, :])
                    step(last)
                    V.memset(rstd[:, w, :, :], 0.0)
                    for i in range(NP):
                        last = V.bn_aggr(mv[:, w, i, :], stats[:, i, :])
                    step(last)
                    V.tensor_scalar(rstd[:, w, 0, :], mv[:, w, :, 1], EPS, None, ALU.add).then_inc(ln_stats[w], 1)

                def normalise(w, group, dst, done):
                    dve.wait_ge(rstd_ready[w], group + 1)
                    for i in range(NP):
                        last = V.tensor_scalar(dst[:, i, :], r[:, w % 2, i, :], mv[:, w, i, 0:1],
                                               rstd[:, w, 1, i:i + 1], ALU.subtract, ALU.mult)
                    last.then_inc(done, 1)

                def other_taps(c):
                    dve.wait_ge(tap_ready, (k + 1) * 2 + c + 1)
                    y = batches(xc[:, c, :])
                    for tap in range(1, KC):
                        ins = V.scalar_tensor_tensor(y, rawp[:, c, :, tap:tap + S], conv_w[:, tap, c:c + 1], y,
                                                     ALU.mult, ALU.add)
                        if tap < KC - 1:
                            step_a(ins)
                    ins.then_inc(xc_ready, 1)

                def gate(c):
                    dve.wait_ge(tg_ready, (k + 1) * 2 + c + 1)
                    src = work(f"gate{c}")
                    V.scalar_tensor_tensor(sg[:, nxt, c, :], th[:, c, :], 1.0, src, ALU.add,
                                           ALU.mult).then_inc(bank_read[bank_of(f"gate{c}")], 1)

                def softmax_shift(j):
                    src = work(f"sc{j}").rearrange("p (h s) -> p h s", s=S)
                    step_t(V.tensor_reduce(nmax[:, j % 2, :], src, AX.X, ALU.max, negate=True))
                    if j >= 3:
                        dve.wait_ge(work_ready, ready(f"pt{j - 3}", k))
                    V.tensor_tensor(pr[:, j % 3, :].rearrange("p (h s) -> p h s", s=S), src,
                                    nmax[:, j % 2, :].unsqueeze(2).to_broadcast([P, H // 2, S]),
                                    ALU.add).then_inc(bank_read[6], 1)

                def divide(i):
                    heads = work(f"pv{i}")[:, 0:H * VW].rearrange("p (h d) -> p h d", d=VW)
                    step_t(V.reciprocal(rden[:, i % 2, :], heads[:, :, HD]))
                    V.tensor_tensor(att[:, i, :].rearrange("p (h d) -> p h d", d=HD), heads[:, :, 0:HD],
                                    rden[:, i % 2, :].unsqueeze(2).to_broadcast([P, H, HD]),
                                    ALU.mult).then_inc(bank_read[5], 1)

                def scan(n):
                    dve.wait_ge(exp_ready, (k * NS + n + 1) * 2)
                    dve.wait_ge(dbu_ready, k * NS + n + 1)
                    wait(dve, cs_ready, k * NS + n - 1)
                    V.tensor_tensor_scan(st[:, n % 2, :], da.rearrange("p c r -> p (c r)"), dbu[:, n % 2, :],
                                         0.0, ALU.mult, ALU.add).then_inc(scanned, 1)

                def times_c(n):
                    dve.wait_ge(scanned, k * NS + n + 1)
                    dve.wait_ge(c_ready, k * NS + n + 1)
                    wait(dve, y_added, k * NS + n - 1)
                    V.tensor_tensor(cs[:, n % 2, :].rearrange("p (c r) -> p c r", c=NH2),
                                    st[:, n % 2, :].rearrange("p (c r) -> p c r", c=NH2),
                                    ps[:, C_BANK, :].unsqueeze(1).to_broadcast([P, NH2, R]),
                                    ALU.mult).then_inc(cs_ready, 1)

                def first_a(n):
                    if n == 6:
                        dve.wait_ge(th_ready, k + 2)
                        V.scalar_tensor_tensor(h[:, nxt, :, :], th[:, :, :], 1.0, xc[:, :, :], ALU.add,
                                               ALU.mult).then_inc(h_ready, 1)
                    if n == 9:
                        dve.wait_ge(split_act, (k + 1) * 3 + 1)
                        step_a(V.tensor_copy(rest[:, :], ssp[DTR:SSP, :]))
                        V.tensor_tensor(rest[:, :], rest[:, :], bc3[0:32, nxt, :],
                                        ALU.subtract).then_inc(split_dve, 1)
                    if n == 11:
                        dve.wait_ge(split_act, (k + 1) * 3 + 3)
                        V.tensor_tensor(bc3[64:96, nxt, :], rest[:, :], mid[:, :],
                                        ALU.subtract).then_inc(split_dve, 1)

                def first_t(n):
                    if n == 0:
                        dve.wait_ge(y_added, k * NS)
                        for c in range(NH2):
                            ins = V.scalar_tensor_tensor(yg[:, c, :], h[:, nxt, c, :], d_skip[:, c:c + 1],
                                                         ps[:, Y_BANK + c, :], ALU.mult, ALU.add)
                        step_t(ins)
                        V.tensor_tensor(yg[:, :, :], yg[:, :, :], sg[:, nxt, :, :], ALU.mult).then_inc(yg_ready, 1)
                    if n == 1:
                        src = work("outp")
                        dve.wait_ge(xres_loaded, k * 16)
                        V.tensor_tensor(r[:, 0, :, :], rows(src), x_res[:, :, :], ALU.add).then_inc(bank_read[6], 1)
                        dve.wait_ge(bank_read[6], read("outp", k))
                        statistics(0, step_t)

                def first_u(n):
                    if n == 2:
                        src = work("wo")
                        dve.wait_ge(x1b_ready, k - 1)
                        V.tensor_tensor(r[:, 1, :, :], rows(src), x1b[:, :, :], ALU.add).then_inc(bank_read[6], 1)
                        dve.wait_ge(bank_read[6], read("wo", k))
                        statistics(1, step_u)
                    if n == 5:
                        src = work("ffn")
                        V.tensor_tensor(f[:, :, :], rows(src), bf[:, :].unsqueeze(1).to_broadcast([P, NP, D]),
                                        ALU.add).then_inc(bank_read[7], 1)
                    if n == 12:
                        dve.wait_ge(f_ready, k - 1)
                        step_u(V.tensor_tensor(r[:, 0, :, :], x2[:, :, :], f[:, :, :], ALU.add))
                        statistics(2, step_u)

                def second_a(n):
                    if n in (3, 4):
                        other_taps(n - 3)
                    if n == 13:
                        dve.wait_ge(sp_step, (k + 1) * 3 + 1)
                        V.tensor_scalar(z[:, :, :], z[:, :, :], 0.0, None, ALU.max).then_inc(zr_ready, 1)
                    if n in (14, 15):
                        gate(n - 14)

                def second_t(n):
                    if n == 1:
                        wait(dve, x1b_ready, k - 1)
                        normalise(0, k - 1, x1, x1_ready)
                    if 4 <= n < 4 + NU:
                        softmax_shift(n - 4)
                    if n in (8, 10, 12, 14):
                        divide((n - 8) // 2)

                def second_u(n):
                    if n == 2:
                        normalise(1, k - 2, x2, x2_ready)
                    if n == 12:
                        dve.wait_ge(stored, (k - 1) * 16)
                        normalise(2, k - 2, o, o_ready)

                def second_s(n):
                    if n == 15:
                        src = work("v")
                        for e in range(2):
                            half = slice(e * S, (e + 1) * S)
                            last = V.tensor_tensor(
                                v_bd[half, :, :, e * VW:e * VW + HD],
                                src[half, :].rearrange("p (b c d) -> p b c d", b=NB, d=HD),
                                bv[half, :].rearrange("p (c e d) -> p c e d", e=2, d=HD)[:, :, e, :]
                                .unsqueeze(1).to_broadcast([S, NB, HP, HD]), ALU.add)
                        last.then_inc(bank_read[6], 1)

                for n in range(NS):
                    if "S" in kk:
                        scan(n)
                    if "T" in kk:
                        first_t(n)
                    if "U" in kk:
                        first_u(n)
                    if "A" in kk:
                        first_a(n)
                    if "S" in kk:
                        times_c(n)
                    if "T" in kk:
                        second_t(n)
                    if "U" in kk:
                        second_u(n)
                    if "A" in kk:
                        second_a(n)
                    if "S" in kk:
                        second_s(n)
                assert "A" not in kk or count["a"] == DVE_A, count
                assert "T" not in kk or count["t"] == DVE_T, count
                assert "U" not in kk or count["u"] == DVE_U, count

            over_groups(dve, iteration)

        @block.gpsimd
        def _(pool):
            Q = nc.gpsimd
            Q.memset(ident[:, :], 0.0).then_inc(pool_const, 1)
            Q.memset(k_bd[:, :, :, :], 0.0).then_inc(pool_const, 1)
            Q.memset(v_bd[:, :, :, :], 0.0).then_inc(pool_const, 1)
            Q.memset(rawp[:, :, :, :], 0.0).then_inc(pool_const, 1)
            Q.memset(mhalf[:, :], -0.5).then_inc(pool_const, 1)
            pool.wait_ge(pool_const, 5)
            Q.affine_select(out=ident[:, :], in_=ident[:, :], compare_op=ALU.not_equal, fill=1.0, base=0,
                            pattern=[[-1, P]], channel_multiplier=1).then_inc(pool_const, 1)
            pool.wait_ge(pool_const, POOL_CONSTS)
            pool.wait_ge(consts_in, N_CONSTS * 16)

            def iteration(k, par):
                kk = kinds(k)
                nxt = 1 - par

                def inverse_deviation(w, group):
                    pool.wait_ge(ln_stats[w], group + 1)
                    Q.tensor_tensor(rstd[:, w, 1, :], rstd[:, w, 0, :], mhalf[:, :],
                                    ALU.pow).then_inc(rstd_ready[w], 1)

                def dbu_of(j, group, b_read):
                    pool.wait_ge(bank_read[5], b_read)
                    wait(pool, scanned, group * NS + j - 1)
                    Q.tensor_tensor(dbu[:, j % 2, :].rearrange("p (c r) -> p c r", c=NH2), u[:, :, :],
                                    b_all[:, j % 4, :].unsqueeze(1).to_broadcast([P, NH2, R]),
                                    ALU.mult).then_inc(dbu_ready, 1)

                for n in range(NS):
                    if "T" in kk and n == 1:
                        inverse_deviation(0, k - 1)
                    if "U" in kk and n == 2:
                        inverse_deviation(1, k - 2)
                    if "U" in kk and n == 12:
                        inverse_deviation(2, k - 2)
                    if "S" in kk and n + 1 < NS:
                        dbu_of(n + 1, k, read_b(n + 1, k))
                    if "T" in kk and n == 3:
                        if "U" in kk:
                            pool.wait_ge(bank_read[6], read("wo", k))
                        pool.wait_ge(x1_ready, k)
                        Q.tensor_tensor(x1b[:, :, :], x1[:, :, :], bo[:, :].unsqueeze(1).to_broadcast([P, NP, D]),
                                        ALU.add).then_inc(x1b_ready, 1)
                    if "A" in kk and n == 14:
                        pool.wait_ge(sp_step, (k + 2) * 3)
                        pool.wait_ge(zr_ready, k + 2)
                        Q.tensor_tensor(dt[:, nxt, :, :], z[:, :, :], dt[:, nxt, :, :],
                                        ALU.add).then_inc(dt_ready, 1)
                    if "A" in kk and n == 15:
                        pool.wait_ge(dt_ready, k + 2)
                        pool.wait_ge(h_ready, k + 2)
                        wait(pool, dbu_ready, (k + 1) * NS)
                        Q.tensor_tensor(u[:, :, :], dt[:, nxt, :, :], h[:, nxt, :, :],
                                        ALU.mult).then_inc(u_ready, 1)
                        pool.wait_ge(u_ready, k + 2)
                        dbu_of(0, k + 1, read("B0", k))

            over_groups(pool, iteration)


N_CONSTS = 26
POOL_CONSTS = 6
ACT_CONSTS = 7
DVE_CONSTS = 12
DVE_A = 5
DVE_T = 15
DVE_U = 5


_INS = ["x", "ctx_1024", "mask_1x1xSxS2_ik0", "L0_attn_W_in", "L0_attn_conv_w", "L0_attn_conv_b", "L0_attn_W_x",
        "L0_attn_W_dt", "L0_attn_b_dt", "L0_attn_A_log", "L0_attn_D", "L0_attn_W_out", "L0_xattn_Wq",
        "L0_xattn_bq", "L0_xattn_Wk", "L0_xattn_bk", "L0_xattn_Wv", "L0_xattn_bv", "L0_xattn_Wo", "L0_xattn_bo",
        "L0_ffn_weight", "L0_ffn_aux_weight1", "L0_ffn_aux_weight2", "L0_ffn_bias"]


def kernel(**inputs):
    import numpy as _np
    import concourse.bacc as _bacc
    from concourse import mybir as _mybir
    from concourse.bass_utils import run_bass_kernel_spmd as _run

    nc = _bacc.Bacc("TRN2", target_bir_lowering=False, num_devices=1)
    arrays, args = {}, {}
    for name in _INS:
        a = _np.ascontiguousarray(inputs[name])
        arrays[f"in_{name}_dram"] = a
        args[name] = nc.dram_tensor(f"in_{name}_dram", a.shape, _mybir.dt.from_np(a.dtype), kind="ExternalInput").ap()
    out = nc.dram_tensor("out_0_dram", inputs["x"].shape, _mybir.dt.float32, kind="ExternalOutput").ap()
    decoder_layer(nc, args, out)
    r = _run(nc, [arrays], core_ids=[0])
    return r.results[0]["out_0_dram"]
```

```python
import numpy as np
import concourse.bass as bass
from concourse import mybir
from contextlib import ExitStack


def decoder_layer(nc, t, out_dram):
    F32, BF16, I32 = mybir.dt.float32, mybir.dt.bfloat16, mybir.dt.int32
    ALU, ACT, AX = mybir.AluOpType, mybir.ActivationFunctionType, mybir.AxisListType

    B, S, D = t["x"].shape
    P = 128
    NB = 8
    R = NB * S
    G = B // NB
    NP = R // P
    CH = t["L0_attn_W_out"].shape[0]
    NH2 = CH // P
    NS = t["L0_attn_A_log"].shape[1]
    KC = t["L0_attn_conv_w"].shape[0]
    DTR = t["L0_attn_W_dt"].shape[0]
    SSP = DTR + 2 * NS
    H = 16
    HD = D // H
    HP = H // 2
    NU = 2 * NP
    SP_ = KC - 1 + S
    VW = HD + 1
    EPS = 1e-5
    NEG = -1.0e30
    QSCALE = float(HD) ** -0.5
    assert R == 512 and NH2 == 2 and NP == 4 and SSP == 96 and SSP - DTR == 32 and NS == 16 and G % 2 == 0

    DA_BANK, C_BANK, Y_BANK = 0, 2, 3
    PIECES = [
        [("xtr", 5, "A"), ("atr", 6, "U")],
        [("outp", 7, "T"), ("raw0", 5, "A"), ("ctr", 6, "S")],
        [("wo", 7, "U"), ("raw1", 6, "A"), ("x1tr", 5, "T")],
        [("kT", 7, "S"), ("qT", 6, "T")],
        [("sc0", 6, "T")],
        [("sc1", 6, "T"), ("x2tr", 5, "U")],
        [("sc2", 6, "T"), ("ffn", 5, "U"), ("pt0", 7, "T")],
        [("sc3", 6, "T"), ("pt1", 7, "T"), ("ssp", 5, "A")],
        [("sc4", 6, "T"), ("pt2", 7, "T"), ("dt0", 5, "A")],
        [("sc5", 6, "T"), ("pt3", 7, "T"), ("pv0", 5, "T")],
        [("sc6", 6, "T"), ("pt4", 7, "T"), ("dt1", 5, "A")],
        [("sc7", 6, "T"), ("pt5", 7, "T"), ("pv1", 5, "T")],
        [("pt6", 7, "T")],
        [("gate0", 6, "A"), ("pt7", 7, "T"), ("pv2", 5, "T")],
        [("gate1", 7, "A"), ("pv3", 5, "T")],
        [("v", 6, "S")]]
    JOBS = [piece for slot in PIECES for piece in slot]

    def kinds(k):
        if not isinstance(k, int):
            return "SATU"
        return "".join(c for c, first in (("A", -1), ("S", 0), ("T", 1), ("U", 2)) if first <= k < first + G)

    def jobs(k, bank=None):
        return [j for j in JOBS if j[2] in kinds(k) and bank in (None, j[1])]

    def before(k, bank=None):
        if isinstance(k, int):
            return sum(len(jobs(i, bank)) for i in range(-1, k))
        return (k - 2) * len(jobs(2, bank)) + before(2, bank)

    def bank_of(name):
        return next(j[1] for j in JOBS if j[0] == name)

    def ready(name, k):
        return before(k) + [j[0] for j in jobs(k)].index(name) + 1

    def read(name, k):
        bank = bank_of(name)
        return before(k, bank) + [j[0] for j in jobs(k, bank)].index(name) + 1

    def wait(eng, semaphore, value):
        if not (isinstance(value, int) and value <= 0):
            eng.wait_ge(semaphore, value)

    ctx = ExitStack()
    with ctx:
        def sb(name, shape, dt=F32):
            return ctx.enter_context(nc.sbuf_tensor(name, shape, dt))

        def sem(name):
            return ctx.enter_context(nc.semaphore(name))

        ident = sb("ident", [P, P])
        identb = sb("identb", [P, P], BF16)
        sel = sb("sel", [SSP, NS, P], BF16)
        mhalf = sb("mhalf", [P, NP])
        maski = sb("maski", [P, S], I32)
        maskneg = sb("maskneg", [P, S], BF16)
        w_in = sb("w_in", [P, 2 * CH])
        conv_w = sb("conv_w", [P, KC, NH2])
        conv_b = sb("conv_b", [P, NH2])
        w_x = sb("w_x", [P, NH2, SSP])
        w_dt = sb("w_dt", [SSP, CH])
        b_dt = sb("b_dt", [P, NH2])
        a_neg = sb("a_neg", [P, NH2, NS])
        d_skip = sb("d_skip", [P, NH2])
        w_out = sb("w_out", [P, NH2, D])
        wraw = sb("wraw", [P, 7, D])
        wT = sb("wT", [P, 6, D])
        w_ffn = sb("w_ffn", [P, 2, D])
        bq = sb("bq", [P, 1])
        bk = sb("bk", [P, 1])
        bv = sb("bv", [P, 1])
        bv_cols = sb("bv_cols", [P, P])
        bo = sb("bo", [P, D])
        bf = sb("bf", [P, D])
        x_in = sb("x_in", [P, NP, D])
        ctx_in = sb("ctx_in", [P, NP, D])
        xT = sb("xT", [P, R])
        ctxT = sb("ctxT", [P, R])
        kT = sb("kT", [P, NB, S])
        k_bd = sb("k_bd", [P, NB, H, S])
        v_bd = sb("v_bd", [P, NB, HP, 2 * VW])
        rawp = sb("rawp", [P, NH2, NB, SP_])
        xc = sb("xc", [P, NH2, R])
        th = sb("th", [P, NH2, R])
        h = sb("h", [P, 2, NH2, R])
        sg = sb("sg", [P, 2, NH2, R])
        ssp = sb("ssp", [SSP, R])
        bc = sb("bc", [2 * NS, 2, R])
        bc3 = sb("bc3", [SSP, 2, R], BF16)
        rest = sb("rest", [32, R])
        mid = sb("mid", [32, R], BF16)
        z = sb("z", [P, NH2, R])
        dt = sb("dt", [P, 2, NH2, R])
        u = sb("u", [P, NH2, R])
        b_all = sb("b_all", [P, 4, R])
        dbu = sb("dbu", [P, 2, NH2 * R])
        st = sb("st", [P, 2, NH2 * R])
        cs = sb("cs", [P, 2, NH2 * R])
        yg = sb("yg", [P, NH2, R])
        x_res = sb("x_res", [P, NP, D])
        r = sb("r", [P, 2, NP, D])
        stats = sb("stats", [P, NP, 6])
        mv = sb("mv", [P, 3, NP, 2])
        rstd = sb("rstd", [P, 3, 2, NP])
        x1 = sb("x1", [P, NP, D])
        x1b = sb("x1b", [P, NP, D])
        x1T = sb("x1T", [P, R])
        qT = sb("qT", [P, R])
        nmax = sb("nmax", [P, 2, H // 2])
        pr = sb("pr", [P, 3, R])
        prT = sb("prT", [P, 3, R])
        rden = sb("rden", [P, 2, H])
        att = sb("att", [P, NP, D])
        attT = sb("attT", [P, R])
        x2 = sb("x2", [P, NP, D])
        x2T = sb("x2T", [P, R])
        f = sb("f", [P, NP, D])
        o = sb("o", [P, NP, D])
        ps = ctx.enter_context(nc.psum_tensor("ps", [P, 8, 512], F32))
        da = ps[:, DA_BANK:DA_BANK + 2, :]

        consts_in = sem("consts_in")
        x_loaded, ctx_loaded, xres_loaded = sem("x_loaded"), sem("ctx_loaded"), sem("xres_loaded")
        kbd_loaded = sem("kbd_loaded")
        b_loaded = [sem(f"b{i}_loaded") for i in range(4)]
        stored = sem("stored")
        pool_const, act_const, dve_const, pe_const = (sem("pool_const"), sem("act_const"), sem("dve_const"),
                                                      sem("pe_const"))
        work_ready = sem("work_ready")
        c_ready = sem("c_ready")
        y_added = sem("y_added")
        bank_read = {5: sem("bank5_read"), 6: sem("bank6_read"), 7: sem("bank7_read")}
        y_based = sem("y_based")
        tap_ready = sem("tap_ready")
        th_ready = sem("th_ready")
        tg_ready = sem("tg_ready")
        sp_step = sem("sp_step")
        split_act = sem("split_act")
        exp_ready = sem("exp_ready")
        f_ready = sem("f_ready")
        pr_ready = sem("pr_ready")
        dve_t, dve_u = sem("dve_t"), sem("dve_u")
        bv_ready = sem("bv_ready")
        conv_step = sem("conv_step")
        max_ready = sem("max_ready")
        xc_ready = sem("xc_ready")
        h_ready = sem("h_ready")
        bc_ready = sem("bc_ready")
        split_dve = sem("split_dve")
        scanned = sem("scanned")
        cs_ready = sem("cs_ready")
        yg_ready = sem("yg_ready")
        ln_stats = [sem(f"ln{i}_stats") for i in range(3)]
        x1_ready, x2_ready, o_ready = sem("x1_ready"), sem("x2_ready"), sem("o_ready")
        dt_ready = sem("dt_ready")
        taps_added = sem("taps_added")
        u_ready = sem("u_ready")
        dbu_ready = sem("dbu_ready")
        rstd_ready = [sem(f"ln{i}_rstd") for i in range(3)]
        x1b_ready = sem("x1b_ready")
        fbias_ready = sem("fbias_ready")
        r3_ready = sem("r3_ready")

        x_rows = t["x"].rearrange("(g i b) s d -> g (b s) i d", g=G, i=NP)
        ctx_rows = t["ctx_1024"].rearrange("(g i b) s d -> g (b s) i d", g=G, i=NP)
        out_rows = out_dram.rearrange("(g i b) s d -> g (b s) i d", g=G, i=NP)

        def over_groups(eng, iteration):
            for k in (-1, 0, 1):
                iteration(k, k % 2)
            with eng.Fori(2, G - 3, 2) as k:
                iteration(k, 0)
                iteration(k + 1, 1)
            for k in range(G - 2, G + 2):
                iteration(k, k % 2)

        block = ctx.enter_context(nc.Block())

        @block.sync
        def _(sp):
            col = lambda a: a.rearrange("(p o) -> p o", o=1)
            row = lambda a: a.rearrange("(o n) -> o n", o=1).to_broadcast([P, D])
            loads = [(w_in[:, :], t["L0_attn_W_in"]),
                     (w_x[:, :, :], t["L0_attn_W_x"].rearrange("(c p) n -> p c n", p=P)),
                     (w_dt[0:DTR, :], t["L0_attn_W_dt"]),
                     (conv_b[:, :], t["L0_attn_conv_b"].rearrange("(c p) -> p c", p=P)),
                     (b_dt[:, :], t["L0_attn_b_dt"].rearrange("(c p) -> p c", p=P)),
                     (d_skip[:, :], t["L0_attn_D"].rearrange("(c p) -> p c", p=P)),
                     (a_neg[:, :, :], t["L0_attn_A_log"].rearrange("(c p) n -> p c n", p=P)),
                     (w_out[:, :, :], t["L0_attn_W_out"].rearrange("(c p) n -> p c n", p=P)),
                     (bq[:, :], col(t["L0_xattn_bq"])), (bk[:, :], col(t["L0_xattn_bk"])),
                     (bv[:, :], col(t["L0_xattn_bv"])), (bo[:, :], row(t["L0_xattn_bo"])),
                     (bf[:, :], row(t["L0_ffn_bias"])),
                     (maski[0:S, :], t["mask_1x1xSxS2_ik0"][0, 0]),
                     (maski[S:2 * S, :], t["mask_1x1xSxS2_ik0"][0, 0])]
            loads += [(conv_w[:, k, :], t["L0_attn_conv_w"][k, 0].rearrange("(c p) -> p c", p=P)) for k in range(KC)]
            loads += [(wraw[:, i, :], t[n]) for i, n in enumerate(
                ("L0_xattn_Wq", "L0_xattn_Wk", "L0_xattn_Wv", "L0_xattn_Wo",
                 "L0_ffn_weight", "L0_ffn_aux_weight1", "L0_ffn_aux_weight2"))]
            assert len(loads) == N_CONSTS
            sp.dma_start(x_in[:, :, :], x_rows[0]).then_inc(x_loaded, 16)
            sp.dma_start(ctx_in[:, :, :], ctx_rows[0]).then_inc(ctx_loaded, 16)
            with nc.allow_non_contiguous_dma(reason="channels of small vectors go to the partitions"):
                for dst, src in loads:
                    sp.dma_start(dst, src).then_inc(consts_in, 16)

            def iteration(k, par):
                kk = kinds(k)
                static = isinstance(k, int)
                nxt = 1 - par

                def load_b(j, parity):
                    sp.dma_start(b_all[:, j % 4, :], bc[j:j + 1, parity, :].unsqueeze(1).to_broadcast([1, P, R])
                                 ).then_inc(b_loaded[j % 4], 16)

                def load_keys(first):
                    for hh in range(first, first + 4):
                        sp.dma_start(k_bd[hh * HD:(hh + 1) * HD, :, hh, :],
                                     kT[hh * HD:(hh + 1) * HD, :, :]).then_inc(kbd_loaded, 16)

                for n in range(NS):
                    if "S" in kk:
                        sp.wait_ge(dbu_ready, k * NS + n + 1)
                        if n + 4 < NS:
                            load_b(n + 4, par)
                    if "A" in kk and n + 4 >= NS:
                        if n + 4 == NS:
                            sp.wait_ge(bc_ready, k + 2)
                        load_b(n + 4 - NS, nxt)
                    if n == 1 and "A" in kk and not (static and k + 2 >= G):
                        sp.wait_ge(bank_read[bank_of("xtr")], read("xtr", k))
                        sp.dma_start(x_in[:, :, :], x_rows[k + 2]).then_inc(x_loaded, 16)
                    if n == 2 and "S" in kk:
                        if "T" in kk:
                            sp.wait_ge(bank_read[bank_of("outp")], read("outp", k))
                        sp.dma_start(x_res[:, :, :], x_rows[k]).then_inc(xres_loaded, 16)
                    if n == 3 and "S" in kk and not (static and k + 1 >= G):
                        sp.wait_ge(bank_read[bank_of("ctr")], read("ctr", k))
                        sp.dma_start(ctx_in[:, :, :], ctx_rows[k + 1]).then_inc(ctx_loaded, 16)
                    if "S" in kk and n == 12:
                        sp.wait_ge(bank_read[7], read("kT", k))
                        if "T" in kk:
                            sp.wait_ge(work_ready, ready("sc7", k))
                        if static and k == 0:
                            sp.wait_ge(pool_const, POOL_CONSTS)
                    if "S" in kk and n >= 12:
                        load_keys((n - 12) * 4)
                    if "U" in kk and n == NS - 1:
                        sp.wait_ge(o_ready, k - 1)
                        sp.dma_start(out_rows[k - 2], o[:, :, :]).then_inc(stored, 16)

            over_groups(sp, iteration)
            sp.wait_ge(stored, (G + 1) * 16)

        @block.tensor
        def _(pe):
            mm = nc.tensor.matmul

            pe.wait_ge(consts_in, N_CONSTS * 16)
            pe.wait_ge(pool_const, POOL_CONSTS)
            for i in range(6):
                last = nc.tensor.transpose(ps[:, 4 + i // 4, (i % 4) * P:(i % 4 + 1) * P], wraw[:, i, :], ident[:, :])
            last.then_inc(pe_const, 1)
            pe.wait_ge(act_const, 3)
            pe.wait_ge(bv_ready, 1)
            mm(ps[:, 6, D:2 * D], bv_cols[:, :], wT[:, 3, :], start=True, stop=True)
            mm(ps[:, 6, 0:D], wT[:, 5, :], wraw[:, 6, :], start=True, stop=True).then_inc(pe_const, 1)
            pe.wait_ge(act_const, 4)
            mm(ps[:, 7, 0:D], wT[:, 4, :], w_ffn[:, 0, :], start=True, stop=True).then_inc(pe_const, 1)
            pe.wait_ge(act_const, ACT_CONSTS)
            pe.wait_ge(dve_const, DVE_CONSTS)
            for c in range(NH2):
                last = mm(ps[:, Y_BANK + c, :], identb[:, :], maskneg[:, :].unsqueeze(1).to_broadcast([P, R // S, S]),
                          start=True, stop=True)
            last.then_inc(pe_const, 1)

            def iteration(k, par):
                kk = kinds(k)
                nxt = 1 - par

                def job(name):
                    wait(pe, bank_read[bank_of(name)], read(name, k) - 1)
                    return ps[:, bank_of(name), :]

                def wait_read(name):
                    pe.wait_ge(bank_read[bank_of(name)], read(name, k))

                def transposes(bank, src):
                    for i in range(NP):
                        last = nc.tensor.transpose(bank[:, i * P:(i + 1) * P], src[:, i, :], ident[:, :])
                    last.then_inc(work_ready, 1)

                def rows_times(bank, lhsT, weights):
                    for i in range(NP):
                        last = mm(bank[:, i * D:(i + 1) * D], lhsT[:, i * P:(i + 1) * P], weights,
                                  start=True, stop=True)
                    last.then_inc(work_ready, 1)

                def scores(j):
                    i, c = j // 2, j % 2
                    bank = job(f"sc{j}")
                    if j == 0:
                        wait_read("qT")
                        pe.wait_ge(kbd_loaded, k * H * 16)
                    mm(bank, identb[:, :], maskneg[:, :].unsqueeze(1).to_broadcast([P, H // 2, S]),
                       start=True, stop=False, skip_group_check=True)
                    for b in range(2):
                        last = mm(bank[b * S:(b + 1) * S, :], qT[:, (2 * i + b) * S:(2 * i + b + 1) * S],
                                  k_bd[:, 2 * i + b, c * H // 2:(c + 1) * H // 2, :],
                                  start=False, stop=True, skip_group_check=True)
                    last.then_inc(work_ready, 1)

                def transpose_probs(j):
                    bank = job(f"pt{j}")
                    pe.wait_ge(pr_ready, (k - 1) * NU + j + 1)
                    for c in range(HP // 2):
                        last = nc.tensor.transpose(bank[:, c * P:(c + 1) * P], pr[:, j % 3, c * P:(c + 1) * P],
                                                   ident[:, :])
                    last.then_inc(work_ready, 1)

                def weigh_values(i):
                    bank = job(f"pv{i}")
                    wait_read(f"pt{2 * i + 1}")
                    for c in range(HP):
                        src = prT[:, (2 * i + c // 4) % 3, :]
                        for b in range(2):
                            last = mm(bank[b * S:(b + 1) * S, c * 2 * VW:(c + 1) * 2 * VW],
                                      src[:, (c % 4) * P + b * S:(c % 4) * P + (b + 1) * S],
                                      v_bd[:, 2 * i + b, c, :], start=True, stop=True, skip_group_check=True)
                    last.then_inc(work_ready, 1)

                def add_y(n):
                    for c in range(NH2):
                        last = mm(ps[:, Y_BANK + c, :], ident[:, :], cs[:, n % 2, c * R:(c + 1) * R],
                                  start=False, stop=n == NS - 1, skip_group_check=True)
                    last.then_inc(y_added, 1)

                def piece(name):
                    kind, c = (name[:-1], int(name[-1])) if name[-1].isdigit() else (name, 0)
                    if kind == "xtr":
                        pe.wait_ge(x_loaded, (k + 2) * 16)
                        transposes(job(name), x_in)
                    if kind == "raw":
                        bank = job(name)
                        wait_read("xtr")
                        mm(bank, w_in[:, c * P:(c + 1) * P], xT[:, :], start=True, stop=True).then_inc(work_ready, 1)
                    if kind == "gate":
                        mm(job(name), w_in[:, CH + c * P:CH + (c + 1) * P], xT[:, :],
                           start=True, stop=True).then_inc(work_ready, 1)
                    if kind == "ssp":
                        bank = job(name)
                        pe.wait_ge(h_ready, k + 2)
                        for c in range(NH2):
                            last = mm(bank[0:SSP, :], w_x[:, c, :], h[:, nxt, c, :], start=c == 0, stop=c == NH2 - 1)
                        last.then_inc(work_ready, 1)
                    if kind == "dt":
                        bank = job(name)
                        wait_read("ssp")
                        mm(bank, w_dt[:, c * P:(c + 1) * P], ssp[:, :], start=True, stop=True).then_inc(work_ready, 1)
                    if kind == "ctr":
                        pe.wait_ge(ctx_loaded, (k + 1) * 16)
                        transposes(job(name), ctx_in)
                    if kind == "kT":
                        bank = job(name)
                        wait_read("ctr")
                        mm(bank, wT[:, 1, :], ctxT[:, :], start=True, stop=True).then_inc(work_ready, 1)
                    if kind == "v":
                        bank = job(name)
                        for b in range(NB):
                            for e in range(2):
                                last = mm(bank[e * S:(e + 1) * S, b * HP * HD:(b + 1) * HP * HD],
                                          ctxT[:, b * S:(b + 1) * S],
                                          wT[:, 2, :].rearrange("p (c e d) -> p c e d", e=2, d=HD)[:, :, e, :],
                                          start=True, stop=True, skip_group_check=True)
                        last.then_inc(work_ready, 1)
                    if kind == "outp":
                        bank = job(name)
                        pe.wait_ge(yg_ready, k)
                        for i in range(NP):
                            for c in range(NH2):
                                last = mm(bank[:, i * D:(i + 1) * D], yg[:, c, i * P:(i + 1) * P], w_out[:, c, :],
                                          start=c == 0, stop=c == NH2 - 1)
                        last.then_inc(work_ready, 1)
                    if kind == "x1tr":
                        bank = job(name)
                        pe.wait_ge(x1_ready, k)
                        transposes(bank, x1)
                    if kind == "qT":
                        bank = job(name)
                        wait_read("x1tr")
                        mm(bank, wT[:, 0, :], x1T[:, :], start=True, stop=True).then_inc(work_ready, 1)
                    if kind == "sc":
                        scores(c)
                    if kind == "pt":
                        transpose_probs(c)
                    if kind == "pv":
                        weigh_values(c)
                    if kind == "atr":
                        bank = job(name)
                        pe.wait_ge(bank_read[5], before(k, 5))
                        transposes(bank, att)
                    if kind == "wo":
                        bank = job(name)
                        wait_read("atr")
                        rows_times(bank, attT, wT[:, 3, :])
                    if kind == "x2tr":
                        bank = job(name)
                        pe.wait_ge(x2_ready, k - 1)
                        transposes(bank, x2)
                    if kind == "ffn":
                        bank = job(name)
                        wait_read("x2tr")
                        rows_times(bank, x2T, w_ffn[:, 1, :])

                for n in range(NS):
                    if "S" in kk or ("T" in kk and n == 0):
                        wait(pe, cs_ready, k * NS + n)
                    if "S" in kk:
                        mm(ps[:, C_BANK, :], sel[:, n, :], bc3[:, par, :], start=True,
                           stop=True).then_inc(c_ready, 1)
                    if "T" in kk and n == 0:
                        add_y(NS - 1)
                    if "S" in kk and n > 1:
                        add_y(n - 1)
                    if "A" in kk and n == NS - 1:
                        pe.wait_ge(split_act, (k + 2) * 3)
                        pe.wait_ge(split_dve, (k + 2) * 2)
                    for name, _, kind in PIECES[n]:
                        if kind in kk:
                            piece(name)
                    if "S" in kk and n == 1:
                        pe.wait_ge(y_based, k + 1)
                        add_y(0)

            over_groups(pe, iteration)

        @block.scalar
        def _(act):
            A = nc.scalar.activation

            act.wait_ge(consts_in, N_CONSTS * 16)
            A(a_neg[:, :, :], a_neg[:, :, :], ACT.Exp).then_inc(act_const, 1)
            act.wait_ge(pe_const, 1)
            A(wT[:, 0:4, :], ps[:, 4, :].rearrange("p (i d) -> p i d", i=4), ACT.Copy).then_inc(act_const, 1)
            A(wT[:, 4:6, :], ps[:, 5, 0:2 * D].rearrange("p (i d) -> p i d", i=2), ACT.Copy).then_inc(act_const, 1)
            act.wait_ge(pe_const, 2)
            A(w_ffn[:, 0, :], ps[:, 6, 0:D], ACT.Copy).then_inc(act_const, 1)
            act.wait_ge(pe_const, 3)
            A(w_ffn[:, 1, :], ps[:, 7, 0:D], ACT.Copy).then_inc(act_const, 1)
            A(w_in[:, CH:2 * CH], w_in[:, CH:2 * CH], ACT.Copy, scale=0.5).then_inc(act_const, 1)
            A(bq[:, :], bq[:, :], ACT.Copy, scale=QSCALE).then_inc(act_const, 1)
            act.wait_ge(act_const, ACT_CONSTS)
            act.wait_ge(dve_const, DVE_CONSTS)
            act.wait_ge(pool_const, POOL_CONSTS)
            act.wait_ge(pe_const, 4)

            def batches(ap):
                return ap.rearrange("p (b s) -> p b s", b=NB)

            def iteration(k, par):
                kk = kinds(k)
                nxt = 1 - par

                def work(name):
                    act.wait_ge(work_ready, ready(name, k))
                    return ps[:, bank_of(name), :]

                def copy(name, dst, func=ACT.Copy, **kw):
                    src = work(name)
                    if len(dst.shape) == 3:
                        src = src.rearrange("p (i d) -> p i d", i=dst.shape[1])
                    A(dst, src, func, **kw).then_inc(bank_read[bank_of(name)], 1)

                def exp_da(n):
                    if n == 0:
                        act.wait_ge(dt_ready, k + 1)
                    wait(act, scanned, k * NS + n)
                    for c in range(NH2):
                        A(batches(da[:, c, :])[:, :, 1:], batches(dt[:, par, c, :])[:, :, 1:], ACT.Exp,
                          scale=a_neg[:, c, n:n + 1]).then_inc(exp_ready, 1)

                def first_taps(c):
                    act.wait_ge(bank_read[bank_of(f"raw{c}")], read(f"raw{c}", k))
                    if c == 0:
                        wait(act, h_ready, k + 1)
                        wait(act, bank_read[7], before(k, 7))
                    A(batches(xc[:, c, :]), rawp[:, c, :, 0:S], ACT.Identity, bias=conv_b[:, c:c + 1],
                      scale=conv_w[:, 0, c:c + 1])
                    A(batches(th[:, c, :]), rawp[:, c, :, 1:1 + S], ACT.Copy,
                      scale=conv_w[:, 1, c:c + 1]).then_inc(tap_ready, 1)

                def first(m):
                    if "A" in kk and m == 8:
                        act.wait_ge(work_ready, ready("ssp", k))
                        A(bc[:, nxt, :], ps[DTR:SSP, 5, :], ACT.Copy).then_inc(bc_ready, 1)
                        A(ssp[:, :], ps[0:SSP, 5, :], ACT.Copy).then_inc(bank_read[5], 1)
                    if "S" in kk and m == 4:
                        wait(act, kbd_loaded, k * H * 16)
                        copy("kT", kT[:, :, :], ACT.Identity, bias=bk[:, 0:1])
                    if "A" in kk and m == 7:
                        act.wait_ge(xc_ready, (k + 2) * 2)
                        A(th[:, :, :], xc[:, :, :], ACT.Tanh).then_inc(th_ready, 1)
                    if "A" in kk and m in (9, 11):
                        c = (m - 9) // 2
                        copy(f"dt{c}", z[:, c, :], ACT.Identity, bias=b_dt[:, c:c + 1])
                    if "U" in kk and m == 7:
                        wait(act, o_ready, k - 2)
                        copy("ffn", f[:, :, :])
                    if "T" in kk and m == 0:
                        act.wait_ge(work_ready, before(k))
                        for e in range(2):
                            half = slice(e * S, (e + 1) * S)
                            last = A(v_bd[half, :, :, e * VW:e * VW + HD],
                                     ps[half, bank_of("v"), :].rearrange("p (b c d) -> p b c d", b=NB, d=HD),
                                     ACT.Copy)
                        last.then_inc(bank_read[bank_of("v")], 1)

                def pieces_a(m):
                    if m == 1:
                        copy("xtr", xT[:, :])
                    if m in (2, 3):
                        c = m - 2
                        copy(f"raw{c}", rawp[:, c, :, KC - 1:])
                    if m in (3, 4):
                        first_taps(m - 3)
                    if m == 8:
                        act.wait_ge(bank_read[5], read("ssp", k))
                        A(bc3[0:32, nxt, :], ssp[DTR:SSP, :], ACT.Copy).then_inc(split_act, 1)
                    if m == 10:
                        act.wait_ge(split_dve, (k + 1) * 2 + 1)
                        A(mid[:, :], rest[:, :], ACT.Copy).then_inc(split_act, 1)
                        A(bc3[32:64, nxt, :], rest[:, :], ACT.Copy).then_inc(split_act, 1)
                    if m == 11:
                        act.wait_ge(bank_read[5], read("dt1", k))
                        wait(act, exp_ready, k * NS * 2)
                        A(dt[:, nxt, :, :], z[:, :, :], ACT.Abs).then_inc(sp_step, 1)
                    if m == 12:
                        act.wait_ge(sp_step, (k + 1) * 3 + 1)
                        A(dt[:, nxt, :, :], dt[:, nxt, :, :], ACT.Exp, scale=-1.0).then_inc(sp_step, 1)
                    if m == 13:
                        act.wait_ge(sp_step, (k + 1) * 3 + 2)
                        A(dt[:, nxt, :, :], dt[:, nxt, :, :], ACT.Ln, bias=1.0).then_inc(sp_step, 1)
                    if m in (14, 15):
                        c = m - 14
                        src = work(f"gate{c}")
                        A(th[:, c, :], src, ACT.Tanh).then_inc(tg_ready, 1)

                def pieces_s(m):
                    if m == 1:
                        wait(act, yg_ready, k)
                        for c in range(NH2):
                            last = A(ps[:, Y_BANK + c, :], h[:, par, c, :], ACT.Copy, scale=d_skip[:, c:c + 1])
                        last.then_inc(y_based, 1)
                    if m == 2:
                        copy("ctr", ctxT[:, :])

                def pieces_t(m):
                    if m == 3:
                        copy("x1tr", x1T[:, :])
                    if m == 4:
                        copy("qT", qT[:, :], ACT.Identity, bias=bq[:, 0:1], scale=QSCALE)
                    if 6 <= m < 6 + NU:
                        j = m - 6
                        act.wait_ge(bank_read[bank_of(f"sc{j}")], read(f"sc{j}", k))
                        A(pr[:, j % 3, :], pr[:, j % 3, :], ACT.Exp).then_inc(pr_ready, 1)
                    if 7 <= m < 7 + NU:
                        j = m - 7
                        if j >= 3:
                            act.wait_ge(work_ready, ready(f"pv{(j - 3) // 2}", k))
                        copy(f"pt{j}", prT[:, j % 3, :])

                def pieces_u(m):
                    if m == 1:
                        copy("atr", attT[:, :])
                    if m == 6:
                        copy("x2tr", x2T[:, :])
                    if m == 9:
                        act.wait_ge(fbias_ready, k - 1)
                        A(f[:, :, :], f[:, :, :], ACT.Tanh).then_inc(f_ready, 1)

                for m in range(NS):
                    if "S" in kk:
                        exp_da(m)
                    first(m)
                    if "T" in kk:
                        pieces_t(m)
                    if "A" in kk:
                        pieces_a(m)
                    if "U" in kk:
                        pieces_u(m)
                    if "S" in kk:
                        pieces_s(m)

            over_groups(act, iteration)

        @block.vector
        def _(dve):
            V = nc.vector
            count = {}

            V.memset(da, 0.0).then_inc(dve_const, 1)
            V.memset(o[:, :, :], 0.0).then_inc(stored, 16)
            V.memset(w_dt[DTR:SSP, :], 0.0).then_inc(dve_const, 1)
            dve.wait_ge(pool_const, POOL_CONSTS)
            V.tensor_copy(identb[:, :], ident[:, :]).then_inc(dve_const, 1)
            for e in range(2):
                V.memset(v_bd[e * S:(e + 1) * S, :, :, e * VW + HD:e * VW + HD + 1], 1.0).then_inc(dve_const, 1)
            for j in range(3):
                V.tensor_copy(sel[32 * j:32 * j + 32, :, :],
                              ident[32 * j:32 * j + 32, 32 * j + NS:32 * j + 32].unsqueeze(2)
                              .to_broadcast([32, NS, P])).then_inc(dve_const, 1)
            dve.wait_ge(consts_in, N_CONSTS * 16)
            V.tensor_copy(bv_cols[:, :], bv[:, 0:1].to_broadcast([P, P])).then_inc(bv_ready, 1)
            V.tensor_scalar(maskneg[:, :], maski[:, :], 0, NEG, ALU.is_equal, ALU.mult).then_inc(dve_const, 1)
            V.tensor_scalar(conv_w[:, :, :], conv_w[:, :, :], 0.5, None, ALU.mult).then_inc(dve_const, 1)
            V.tensor_scalar(conv_b[:, :], conv_b[:, :], 0.5, None, ALU.mult).then_inc(dve_const, 1)
            dve.wait_ge(act_const, ACT_CONSTS)
            dve.wait_ge(pe_const, 2)
            V.tensor_tensor(bo[:, :], bo[:, :], ps[:, 6, D:2 * D], ALU.add).then_inc(dve_const, 1)
            V.tensor_scalar(a_neg[:, :, :], a_neg[:, :, :], -1.0, None, ALU.mult).then_inc(dve_const, 1)
            dve.wait_ge(dve_const, DVE_CONSTS)

            def batches(ap):
                return ap.rearrange("p (b s) -> p b s", b=NB)

            def iteration(k, par):
                kk = kinds(k)
                nxt = 1 - par
                count["t"] = count["u"] = 0

                def step_t(ins):
                    count["t"] += 1
                    ins.then_inc(dve_t, 1)
                    dve.wait_ge(dve_t, (k - 1) * DVE_T + count["t"])

                def step_u(ins):
                    count["u"] += 1
                    ins.then_inc(dve_u, 1)
                    dve.wait_ge(dve_u, (k - 2) * DVE_U + count["u"])

                def work(name):
                    dve.wait_ge(work_ready, ready(name, k))
                    return ps[:, bank_of(name), :]

                def rows(bank):
                    return bank.rearrange("p (i d) -> p i d", i=NP)

                def statistics(w, src, step):
                    for i in range(NP):
                        last = V.bn_stats(stats[:, i, :], src[:, i, :])
                    step(last)
                    V.memset(rstd[:, w, :, :], 0.0)
                    for i in range(NP):
                        last = V.bn_aggr(mv[:, w, i, :], stats[:, i, :])
                    step(last)
                    V.tensor_scalar(rstd[:, w, 0, :], mv[:, w, :, 1], EPS, None, ALU.add).then_inc(ln_stats[w], 1)

                def normalise(w, group, src, dst, done):
                    dve.wait_ge(rstd_ready[w], group + 1)
                    for i in range(NP):
                        last = V.tensor_scalar(dst[:, i, :], src[:, i, :], mv[:, w, i, 0:1],
                                               rstd[:, w, 1, i:i + 1], ALU.subtract, ALU.mult)
                    last.then_inc(done, 1)

                def tap(c, number):
                    if number == 2:
                        dve.wait_ge(taps_added, (k + 1) * 2 + c + 1)
                    else:
                        dve.wait_ge(conv_step, (k + 1) * NH2 + c + 1)
                    y = batches(xc[:, c, :])
                    V.scalar_tensor_tensor(y, rawp[:, c, :, number:number + S], conv_w[:, number, c:c + 1], y,
                                           ALU.mult, ALU.add).then_inc(xc_ready if number == KC - 1 else conv_step, 1)

                def gate(c):
                    dve.wait_ge(tg_ready, (k + 1) * 2 + c + 1)
                    src = work(f"gate{c}")
                    V.scalar_tensor_tensor(sg[:, nxt, c, :], th[:, c, :], 1.0, src, ALU.add,
                                           ALU.mult).then_inc(bank_read[bank_of(f"gate{c}")], 1)

                def unit_max(j):
                    src = work(f"sc{j}").rearrange("p (h s) -> p h s", s=S)
                    V.tensor_reduce(nmax[:, j % 2, :], src, AX.X, ALU.max, negate=True).then_inc(max_ready, 1)

                def subtract_max(j):
                    dve.wait_ge(max_ready, (k - 1) * NU + j + 1)
                    if j >= 3:
                        dve.wait_ge(work_ready, ready(f"pt{j - 3}", k))
                    bank = bank_of(f"sc{j}")
                    V.tensor_tensor(pr[:, j % 3, :].rearrange("p (h s) -> p h s", s=S),
                                    ps[:, bank, :].rearrange("p (h s) -> p h s", s=S),
                                    nmax[:, j % 2, :].unsqueeze(2).to_broadcast([P, H // 2, S]),
                                    ALU.add).then_inc(bank_read[bank], 1)

                def divide(i):
                    heads = work(f"pv{i}")[:, 0:H * VW].rearrange("p (h d) -> p h d", d=VW)
                    step_t(V.reciprocal(rden[:, i % 2, :], heads[:, :, HD]))
                    V.tensor_tensor(att[:, i, :].rearrange("p (h d) -> p h d", d=HD), heads[:, :, 0:HD],
                                    rden[:, i % 2, :].unsqueeze(2).to_broadcast([P, H, HD]),
                                    ALU.mult).then_inc(bank_read[bank_of(f"pv{i}")], 1)

                def scan(n):
                    dve.wait_ge(exp_ready, (k * NS + n + 1) * 2)
                    dve.wait_ge(dbu_ready, k * NS + n + 1)
                    wait(dve, cs_ready, k * NS + n - 1)
                    V.tensor_tensor_scan(st[:, n % 2, :], da.rearrange("p c r -> p (c r)"), dbu[:, n % 2, :],
                                         0.0, ALU.mult, ALU.add).then_inc(scanned, 1)

                def times_c(n):
                    dve.wait_ge(scanned, k * NS + n + 1)
                    dve.wait_ge(c_ready, k * NS + n + 1)
                    wait(dve, y_added, k * NS + n - 1)
                    V.tensor_tensor(cs[:, n % 2, :].rearrange("p (c r) -> p c r", c=NH2),
                                    st[:, n % 2, :].rearrange("p (c r) -> p c r", c=NH2),
                                    ps[:, C_BANK, :].unsqueeze(1).to_broadcast([P, NH2, R]),
                                    ALU.mult).then_inc(cs_ready, 1)

                def first_a(n):
                    if n == 4:
                        tap(0, 2)
                    if n in (5, 6):
                        tap(n - 5, 3)
                    if n == 7:
                        dve.wait_ge(th_ready, k + 2)
                        V.scalar_tensor_tensor(h[:, nxt, :, :], th[:, :, :], 1.0, xc[:, :, :], ALU.add,
                                               ALU.mult).then_inc(h_ready, 1)
                    if n == 9:
                        dve.wait_ge(split_act, (k + 1) * 3 + 1)
                        V.tensor_tensor(rest[:, :], bc[:, nxt, :], bc3[0:32, nxt, :],
                                        ALU.subtract).then_inc(split_dve, 1)
                    if n == 11:
                        dve.wait_ge(split_act, (k + 1) * 3 + 3)
                        V.tensor_tensor(bc3[64:96, nxt, :], rest[:, :], mid[:, :],
                                        ALU.subtract).then_inc(split_dve, 1)
                    if n == 14:
                        dve.wait_ge(sp_step, (k + 2) * 3)
                        V.scalar_tensor_tensor(dt[:, nxt, :, :], z[:, :, :], 0.0, dt[:, nxt, :, :], ALU.max,
                                               ALU.add).then_inc(dt_ready, 1)
                    if n == 15:
                        gate(0)

                def first_t(n):
                    if n == 2:
                        wait(dve, x1b_ready, k - 1)
                        normalise(0, k - 1, r[:, 0, :, :], x1, x1_ready)
                    if 5 <= n < 5 + NU:
                        subtract_max(n - 5)
                    if n in (10, 12, 14, 15):
                        divide((10, 12, 14, 15).index(n))

                def first_u(n):
                    if n == 3:
                        dve.wait_ge(bank_read[7], read("wo", k))
                        statistics(1, r[:, 1, :, :], step_u)

                def second_a(n):
                    if n == 5:
                        tap(1, 2)
                    if n == 15:
                        gate(1)

                def second_t(n):
                    if n == 0:
                        dve.wait_ge(y_added, k * NS)
                        V.tensor_tensor(yg[:, :, :], ps[:, Y_BANK:Y_BANK + 2, :], sg[:, nxt, :, :],
                                        ALU.mult).then_inc(yg_ready, 1)
                    if n == 1:
                        src = work("outp")
                        dve.wait_ge(xres_loaded, k * 16)
                        V.tensor_tensor(r[:, 0, :, :], rows(src), x_res[:, :, :],
                                        ALU.add).then_inc(bank_read[bank_of("outp")], 1)
                        dve.wait_ge(bank_read[bank_of("outp")], read("outp", k))
                        statistics(0, r[:, 0, :, :], step_t)
                    if 4 <= n < 4 + NU:
                        unit_max(n - 4)

                def second_u(n):
                    if n == 2:
                        src = work("wo")
                        dve.wait_ge(x1b_ready, k - 1)
                        V.tensor_tensor(r[:, 1, :, :], rows(src), x1b[:, :, :], ALU.add).then_inc(bank_read[7], 1)
                    if n == 3:
                        wait(dve, r3_ready, k - 2)
                        normalise(1, k - 2, r[:, 1, :, :], x2, x2_ready)
                    if n == 12:
                        dve.wait_ge(r3_ready, k - 1)
                        statistics(2, f, step_u)
                    if n == 13:
                        dve.wait_ge(stored, (k - 1) * 16)
                        normalise(2, k - 2, f, o, o_ready)

                for n in range(NS):
                    if "S" in kk:
                        scan(n)
                    if "T" in kk:
                        first_t(n)
                    if "U" in kk:
                        first_u(n)
                    if "A" in kk:
                        first_a(n)
                    if "S" in kk:
                        times_c(n)
                    if "T" in kk:
                        second_t(n)
                    if "U" in kk:
                        second_u(n)
                    if "A" in kk:
                        second_a(n)
                assert "T" not in kk or count["t"] == DVE_T, count
                assert "U" not in kk or count["u"] == DVE_U, count

            over_groups(dve, iteration)

        @block.gpsimd
        def _(pool):
            Q = nc.gpsimd
            Q.memset(ident[:, :], 0.0).then_inc(pool_const, 1)
            Q.memset(k_bd[:, :, :, :], 0.0).then_inc(pool_const, 1)
            Q.memset(v_bd[:, :, :, :], 0.0).then_inc(pool_const, 1)
            Q.memset(rawp[:, :, :, :], 0.0).then_inc(pool_const, 1)
            Q.memset(mhalf[:, :], -0.5).then_inc(pool_const, 1)
            pool.wait_ge(pool_const, 5)
            Q.affine_select(out=ident[:, :], in_=ident[:, :], compare_op=ALU.not_equal, fill=1.0, base=0,
                            pattern=[[-1, P]], channel_multiplier=1).then_inc(pool_const, 1)
            pool.wait_ge(pool_const, POOL_CONSTS)
            pool.wait_ge(consts_in, N_CONSTS * 16)
            pool.wait_ge(dve_const, DVE_CONSTS)

            def iteration(k, par):
                kk = kinds(k)
                nxt = 1 - par

                def inverse_deviation(w, group):
                    pool.wait_ge(ln_stats[w], group + 1)
                    Q.tensor_tensor(rstd[:, w, 1, :], rstd[:, w, 0, :], mhalf[:, :],
                                    ALU.pow).then_inc(rstd_ready[w], 1)

                def dbu_of(j, group):
                    pool.wait_ge(b_loaded[j % 4], (group * (NS // 4) + j // 4 + 1) * 16)
                    wait(pool, scanned, group * NS + j - 1)
                    Q.tensor_tensor(dbu[:, j % 2, :].rearrange("p (c r) -> p c r", c=NH2), u[:, :, :],
                                    b_all[:, j % 4, :].unsqueeze(1).to_broadcast([P, NH2, R]),
                                    ALU.mult).then_inc(dbu_ready, 1)

                for n in range(NS):
                    if "S" in kk and n + 1 < NS:
                        dbu_of(n + 1, k)
                    if "T" in kk and n == 1:
                        inverse_deviation(0, k - 1)
                    if "U" in kk and n == 3:
                        inverse_deviation(1, k - 2)
                    if "A" in kk and n in (3, 4):
                        c = n - 3
                        pool.wait_ge(tap_ready, (k + 1) * 2 + c + 1)
                        Q.tensor_tensor(xc[:, c, :], xc[:, c, :], th[:, c, :], ALU.add).then_inc(taps_added, 1)
                    if "T" in kk and n == 3:
                        if "U" in kk:
                            pool.wait_ge(bank_read[7], read("wo", k))
                        pool.wait_ge(x1_ready, k)
                        Q.tensor_tensor(x1b[:, :, :], x1[:, :, :], bo[:, :].unsqueeze(1).to_broadcast([P, NP, D]),
                                        ALU.add).then_inc(x1b_ready, 1)
                    if "U" in kk and n == 7:
                        pool.wait_ge(bank_read[5], read("ffn", k))
                        Q.tensor_tensor(f[:, :, :], f[:, :, :], bf[:, :].unsqueeze(1).to_broadcast([P, NP, D]),
                                        ALU.add).then_inc(fbias_ready, 1)
                    if "U" in kk and n == 10:
                        pool.wait_ge(f_ready, k - 1)
                        Q.tensor_tensor(f[:, :, :], x2[:, :, :], f[:, :, :], ALU.add).then_inc(r3_ready, 1)
                    if "U" in kk and n == 12:
                        inverse_deviation(2, k - 2)
                    if "A" in kk and n == 14:
                        pool.wait_ge(dt_ready, k + 2)
                        pool.wait_ge(h_ready, k + 2)
                        wait(pool, dbu_ready, (k + 1) * NS)
                        Q.tensor_tensor(u[:, :, :], dt[:, nxt, :, :], h[:, nxt, :, :],
                                        ALU.mult).then_inc(u_ready, 1)
                    if "A" in kk and n == 15:
                        pool.wait_ge(u_ready, k + 2)
                        dbu_of(0, k + 1)

            over_groups(pool, iteration)


N_CONSTS = 26
POOL_CONSTS = 6
ACT_CONSTS = 7
DVE_CONSTS = 13
DVE_T = 6
DVE_U = 4


_INS = ["x", "ctx_1024", "mask_1x1xSxS2_ik0", "L0_attn_W_in", "L0_attn_conv_w", "L0_attn_conv_b", "L0_attn_W_x",
        "L0_attn_W_dt", "L0_attn_b_dt", "L0_attn_A_log", "L0_attn_D", "L0_attn_W_out", "L0_xattn_Wq",
        "L0_xattn_bq", "L0_xattn_Wk", "L0_xattn_bk", "L0_xattn_Wv", "L0_xattn_bv", "L0_xattn_Wo", "L0_xattn_bo",
        "L0_ffn_weight", "L0_ffn_aux_weight1", "L0_ffn_aux_weight2", "L0_ffn_bias"]


def kernel(**inputs):
    import numpy as _np
    import concourse.bacc as _bacc
    from concourse import mybir as _mybir
    from concourse.bass_utils import run_bass_kernel_spmd as _run

    nc = _bacc.Bacc("TRN2", target_bir_lowering=False, num_devices=1)
    arrays, args = {}, {}
    for name in _INS:
        a = _np.ascontiguousarray(inputs[name])
        arrays[f"in_{name}_dram"] = a
        args[name] = nc.dram_tensor(f"in_{name}_dram", a.shape, _mybir.dt.from_np(a.dtype), kind="ExternalInput").ap()
    out = nc.dram_tensor("out_0_dram", inputs["x"].shape, _mybir.dt.float32, kind="ExternalOutput").ap()
    decoder_layer(nc, args, out)
    r = _run(nc, [arrays], core_ids=[0])
    return r.results[0]["out_0_dram"]
```
